# Optimizing a Trainium2 kernel written in Bass

```python
import numpy as np
import jax
import jax.numpy as jnp

def _softmax(x, axis=-1):
    return jax.nn.softmax(x, axis=axis)

def _gelu(x):
    return jax.nn.gelu(x, approximate=True)

def _silu(x):
    return jax.nn.silu(x)

def _sigmoid(x):
    return jax.nn.sigmoid(x)

def _layernorm(x, axis=-1, eps=1e-05):
    m = jnp.mean(x, axis=axis, keepdims=True)
    v = jnp.var(x, axis=axis, keepdims=True)
    return (x - m) / jnp.sqrt(v + eps)

def _scatter_add(tgt, idx, src, axis=0):
    return tgt.at[idx].add(src)

def _segment_sum(src, seg, n):
    return jax.ops.segment_sum(src, seg, n)
kernel_name = 'mk_macaron_d1_jaxref_r8_f65872'

def setup_inputs(seed: int=0):
    np.random.seed(seed)
    _w = jnp.asarray

    def _L0_attn_setup():
        import jax, jax.numpy as jnp
        import numpy as np
        HEADS = 8
        DIM_HEAD = 128
        ATTN_MATRIX_SCALE = 1.5
        SCALE = DIM_HEAD ** (-0.5)

        def _split_heads(t):
            b, n, _ = t.shape
            t = t.reshape(b, n, HEADS, DIM_HEAD)
            return t.transpose(2, 0, 1, 3).reshape(HEADS, b * n, DIM_HEAD)
        key = jax.random.key(seed)
        ks = jax.random.split(key, 7)
        b, n, m = (2, 256, 256)
        qd, cd, inner = (128, 96, HEADS * DIM_HEAD)
        x = jax.random.normal(ks[0], (b, n, qd), dtype=jnp.float32)
        context = jax.random.normal(ks[1], (b, m, cd), dtype=jnp.float32)
        Wq = jax.random.normal(ks[2], (qd, inner), dtype=jnp.float32) * qd ** (-0.5)
        Wk = jax.random.normal(ks[3], (cd, inner), dtype=jnp.float32) * cd ** (-0.5)
        Wv = jax.random.normal(ks[4], (cd, inner), dtype=jnp.float32) * cd ** (-0.5)
        Wout = jax.random.normal(ks[5], (inner, qd), dtype=jnp.float32) * inner ** (-0.5)
        bout = jnp.zeros((qd,), dtype=jnp.float32)
        return {'x': x, 'context': context, 'Wq': Wq, 'Wk': Wk, 'Wv': Wv, 'Wout': Wout, 'bout': bout}
    _L0_attn_in = _L0_attn_setup()

    def _L0_ffn_setup():
        import jax, jax.numpy as jnp
        import numpy as np
        D_MODEL = 128
        D_FF = 512
        NUM_EXPERTS = 8
        key = jax.random.key(seed)
        ks = jax.random.split(key, 8)
        scale_in = 1.0 / np.sqrt(D_MODEL)
        scale_ff = 1.0 / np.sqrt(D_FF)
        x = jax.random.normal(ks[0], (4, 256, D_MODEL), dtype=jnp.float32)
        gate_w = jax.random.uniform(ks[1], (NUM_EXPERTS, D_MODEL), jnp.float32, -scale_in, scale_in)
        gate_b = jax.random.uniform(ks[2], (NUM_EXPERTS,), jnp.float32, -scale_in, scale_in)
        expert_bias = jnp.zeros((NUM_EXPERTS,), dtype=jnp.float32)
        w1 = jax.random.uniform(ks[3], (NUM_EXPERTS, D_MODEL, D_FF), jnp.float32, -scale_in, scale_in)
        b1 = jax.random.uniform(ks[4], (NUM_EXPERTS, D_FF), jnp.float32, -scale_in, scale_in)
        w2 = jax.random.uniform(ks[5], (NUM_EXPERTS, D_FF, D_MODEL), jnp.float32, -scale_ff, scale_ff)
        b2 = jax.random.uniform(ks[6], (NUM_EXPERTS, D_MODEL), jnp.float32, -scale_ff, scale_ff)
        return {'x': x, 'gate_w': gate_w, 'gate_b': gate_b, 'expert_bias': expert_bias, 'w1': w1, 'b1': b1, 'w2': w2, 'b2': b2}
    _L0_ffn_in = _L0_ffn_setup()
    _d = {'L0_attn_x': _L0_attn_in['x'], 'L0_attn_context': _L0_attn_in['context'], 'L0_attn_Wq': _L0_attn_in['Wq'], 'L0_attn_Wk': _L0_attn_in['Wk'], 'L0_attn_Wv': _L0_attn_in['Wv'], 'L0_attn_Wout': _L0_attn_in['Wout'], 'L0_attn_bout': _L0_attn_in['bout'], 'L0_ffn_gate_w': _L0_ffn_in['gate_w'], 'L0_ffn_gate_b': _L0_ffn_in['gate_b'], 'L0_ffn_expert_bias': _L0_ffn_in['expert_bias'], 'L0_ffn_w1': _L0_ffn_in['w1'], 'L0_ffn_b1': _L0_ffn_in['b1'], 'L0_ffn_w2': _L0_ffn_in['w2'], 'L0_ffn_b2': _L0_ffn_in['b2']}
    _x0 = _d['L0_attn_x']
    _d['L0_attn_x'] = jax.random.normal(jax.random.fold_in(jax.random.key(seed), 1), (16, 256, 128), dtype=_x0.dtype)
    del _x0
    return _d

def reference(L0_attn_x, L0_attn_context, L0_attn_Wq, L0_attn_Wk, L0_attn_Wv, L0_attn_Wout, L0_attn_bout, L0_ffn_gate_w, L0_ffn_gate_b, L0_ffn_expert_bias, L0_ffn_w1, L0_ffn_b1, L0_ffn_w2, L0_ffn_b2):

    def _L0_attn_ref(x, context, Wq, Wk, Wv, Wout, bout):
        import jax, jax.numpy as jnp
        import numpy as np
        HEADS = 8
        DIM_HEAD = 128
        ATTN_MATRIX_SCALE = 1.5
        SCALE = DIM_HEAD ** (-0.5)

        def _split_heads(t):
            b, n, _ = t.shape
            t = t.reshape(b, n, HEADS, DIM_HEAD)
            return t.transpose(2, 0, 1, 3).reshape(HEADS, b * n, DIM_HEAD)
        b, n, _ = x.shape
        qh = _split_heads(jnp.einsum('bnq,qi->bni', x, Wq))
        kh = _split_heads(jnp.einsum('bmc,ci->bmi', context, Wk))
        vh = _split_heads(jnp.einsum('bmc,ci->bmi', context, Wv))
        sim = jnp.einsum('hid,hjd->hij', qh, kh) * SCALE
        mean = jnp.mean(sim, axis=-1, keepdims=True)
        sim = (sim - mean) * ATTN_MATRIX_SCALE + mean
        attn = jax.nn.softmax(sim, axis=-1)
        out = jnp.einsum('hij,hjd->hid', attn, vh)
        out = out.reshape(HEADS, b, n, DIM_HEAD).transpose(1, 2, 0, 3)
        out = out.reshape(b, n, HEADS * DIM_HEAD)
        return jnp.einsum('bni,iq->bnq', out, Wout) + bout

    def _L0_ffn_ref(x, gate_w, gate_b, expert_bias, w1, b1, w2, b2):
        import jax, jax.numpy as jnp
        import numpy as np
        D_MODEL = 128
        D_FF = 512
        NUM_EXPERTS = 8
        gate_logits = jnp.einsum('bsd,ed->bse', x, gate_w) + gate_b + expert_bias
        top_idx = jnp.argmax(gate_logits, axis=-1)
        out = jnp.zeros_like(x)
        for e in range(NUM_EXPERTS):
            mask = (top_idx == e)[..., None].astype(x.dtype)
            h = jax.nn.relu(jnp.einsum('bsd,df->bsf', x, w1[e]) + b1[e])
            y = jnp.einsum('bsf,fd->bsd', h, w2[e]) + b2[e]
            out = out + mask * y
        return out
    x = L0_attn_x
    x = x + 0.5 * _L0_ffn_ref(_layernorm(x, axis=-1), L0_ffn_gate_w, L0_ffn_gate_b, L0_ffn_expert_bias, L0_ffn_w1, L0_ffn_b1, L0_ffn_w2, L0_ffn_b2)
    x = x + _L0_attn_ref(_layernorm(x, axis=-1), L0_attn_context, L0_attn_Wq, L0_attn_Wk, L0_attn_Wv, L0_attn_Wout, L0_attn_bout)
    x = x + 0.5 * _L0_ffn_ref(_layernorm(x, axis=-1), L0_ffn_gate_w, L0_ffn_gate_b, L0_ffn_expert_bias, L0_ffn_w1, L0_ffn_b1, L0_ffn_w2, L0_ffn_b2)
    return x

_drawn_inputs = setup_inputs


def setup_inputs(seed=0):
    import zlib

    import numpy as np

    out = dict(_drawn_inputs(seed))
    spreads = {'L0_attn_bout': (0.0, 0.1), 'L0_ffn_expert_bias': (0.0, 0.1)}
    factors = {}
    for name, (base, spread) in spreads.items():
        noise = np.random.default_rng([zlib.crc32(name.encode()), seed]).standard_normal(out[name].shape)
        drawn = base * np.exp(spread * noise) if base else spread * noise
        out[name] = jnp.asarray(drawn.astype(out[name].dtype))
    for name, factor in factors.items():
        out[name] = (out[name] * factor).astype(out[name].dtype)
    return out
```

```python
import concourse.bass as bass
from concourse import mybir
from contextlib import ExitStack

P = 128
EPS = 1e-05


def macaron_kernel(nc, x, context, Wq, Wk, Wv, Wout, bout, gate_w, gate_b, expert_bias, w1, b1, w2, b2, out):
    fp32, f32r, i32, bf16 = (mybir.dt.float32, mybir.dt.float32r, mybir.dt.int32, mybir.dt.bfloat16)
    ALU = mybir.AluOpType
    ACT = mybir.ActivationFunctionType
    AX = mybir.AxisListType
    ds = bass.ds

    N = x.shape[0] * x.shape[1]
    D = x.shape[2]
    T = N // P
    KEYS = context.shape[0] * context.shape[1]
    KC = KEYS // P
    C = context.shape[2]
    H = Wq.shape[1] // D
    SCALE = float(D) ** -0.5
    SHARPEN = 1.5
    E, F = w1.shape[0], w1.shape[2]
    FC = F // P
    SLOTS = T + E - 1
    G = 4
    NG = T // G
    ROW = D + 3
    ID, MEAN, RSTD = D, D + 1, D + 2

    x_rows = x.rearrange("b n d -> (b n) d").rearrange("(p t) d -> p t d", t=T)
    out_rows = out.rearrange("b n d -> (b n) d")
    x1 = nc.dram_tensor("x1", [N, D], fp32, kind="Internal").ap()
    slots = [nc.dram_tensor(f"slots{r}", [SLOTS * P, ROW], fp32, kind="Internal").ap() for r in range(2)]
    x1_rows = x1.rearrange("(p t) d -> p t d", t=T)
    ffn_dst = [x1, out_rows]

    ctx = ExitStack()
    with ctx:
        def sb(name, shape, dt, where=ctx):
            return where.enter_context(nc.sbuf_tensor(name, shape, dt))

        def sem(name):
            return ctx.enter_context(nc.semaphore(name))

        ROWS = sb("rows", [P, T, ROW], fp32)
        W1H = sb("w1_hi", [P, E, F], f32r)
        W1L = sb("w1_lo", [P, E, F], f32r)
        W2HL = sb("w2_hi_lo", [P, E, FC, 2, D], f32r)
        MH = sb("m_hi", [P, H, KEYS], f32r)
        ML = sb("m_lo", [P, H, KEYS], f32r)
        VWH = sb("vw_hi", [P, H, KC, D], f32r)
        VWL = sb("vw_lo", [P, H, KC, D], f32r)
        XN = sb("xn", [P, G, D], fp32)
        XNT = sb("xnT", [P, G * P], fp32)
        IDN = sb("ident", [P, P], fp32)
        BEFORE = sb("before", [P, P], bf16)
        ONES = sb("ones", [P, P], bf16)
        FILL = sb("fill", [P, ROW], fp32)
        NHALF = sb("nhalf", [P, G], fp32)
        GWR = sb("gate_w", [E, D], fp32)
        GWT = sb("gate_wT", [P, E], fp32)
        GB = sb("gate_b", [P, E], fp32)
        EB = sb("expert_bias", [P, E], fp32)
        BO = sb("bout", [P, 1], fp32)
        PREF = sb("pref", [P, E], fp32)
        TIDX = sb("tile_index", [P, SLOTS], fp32)
        BN = sb("bn", [P, G, 6], fp32)
        MV = sb("mean_var", [P, G, 2], fp32)
        VE = sb("var_eps", [P, G], fp32)
        RS = sb("rstd", [P, G], fp32)
        LG = sb("logits", [P, T, E], fp32)
        MX = sb("row_max", [P, T], fp32)
        OH = sb("onehot", [P, E, T], bf16)
        POS = sb("pos", [P, T], i32)
        CNT = sb("counts", [P, 6, E], fp32)
        CNTI = sb("counts_int", [P, 2, E], i32)
        ET = sb("expert_of_tile", [P, SLOTS], i32)
        ETF = sb("expert_of_tile_f", [P, SLOTS], fp32)
        SEL = sb("sel", [P, SLOTS, E - 1], fp32)
        WRK = sb("route_work", [P, E, T], fp32)
        ONF = sb("ones_f", [P, E * T], fp32)

        with ExitStack() as prep:
            WRAW = sb("w_raw", [P, E * F], fp32, prep)
            CTX = sb("ctx", [P, KC, C], fp32, prep)
            CTXT = sb("ctxT", [C, KEYS], fp32, prep)
            WQR = sb("wq", [P, H, D], fp32, prep)
            WKR = sb("wk", [C, H, D], fp32, prep)
            WVR = sb("wv", [C, H, D], fp32, prep)
            WOR = sb("wout", [P, H, D], fp32, prep)
            WQT = sb("wqT", [P, P], fp32, prep)
            KT = sb("kT", [P, KEYS], fp32, prep)
            VT = sb("vT", [P, KEYS], fp32, prep)
            MT = sb("m_tmp", [P, KEYS], fp32, prep)
            SM = sb("m_sum", [P, 2], fp32, prep)
        with ExitStack() as ffn:
            B1 = sb("b1", [P, E, F], fp32, ffn)
            B2 = sb("b2", [P, E, D], fp32, ffn)
            NX = 6
            XS = sb("slot_rows", [P, NX, ROW], fp32, ffn)
            RES = sb("result_rows", [P, NX, D], fp32, ffn)
            IDS = sb("result_ids", [P, NX], i32, ffn)
            XSN = sb("slot_xn", [P, 2, D], fp32, ffn)
            XTH = sb("slot_xT_hi", [P, 2, P], f32r, ffn)
            XTL = sb("slot_xT_lo", [P, 2, P], f32r, ffn)
            HB = sb("h", [P, 2, F], fp32, ffn)
            HTH = sb("hT_hi", [P, 2, FC * P], f32r, ffn)
            HTL = sb("hT_lo", [P, 2, FC * P], f32r, ffn)
            XB = sb("x_b2", [P, 2, D], fp32, ffn)
            YT = sb("y_part", [P, 2, D], fp32, ffn)
        with ExitStack() as att:
            PTH = sb("probsT_hi", [P, 2, KC, G * P], f32r, att)
            PTL = sb("probsT_lo", [P, 2, KC, G * P], f32r, att)
            PR = sb("probs", [P, 4, KEYS], fp32, att)
            AXH = sb("xT_hi", [P, 2, G * P], f32r, att)
            AXL = sb("xT_lo", [P, 2, G * P], f32r, att)
            OT = sb("oT", [P, G * P], fp32, att)
            NM = sb("neg_max", [P, 4], fp32, att)
            SU = sb("row_sum", [P, 4], fp32, att)
            RI = sb("row_inv", [P, 4], fp32, att)

        BK = [ctx.enter_context(nc.psum_tensor(f"bank{i}", [P, 512], fp32)) for i in range(8)]

        x_in = sem("x_in")
        small_in = sem("small_in")
        w1_in, w2_in = sem("w1_in"), sem("w2_in")
        attw_in = sem("attw_in")
        slots_filled = sem("slots_filled")
        zeroed = sem("zeroed")
        consts_ready = sem("consts_ready")
        fill_ready = sem("fill_ready")
        gate_ps, gate_ready = sem("gate_ps"), sem("gate_ready")
        w_hi, w_lo = sem("w_hi"), sem("w_lo")
        ctxT_ps, ctxT_ready = sem("ctxT_ps"), sem("ctxT_ready")
        prep_qk_ps, prep_v_ps = sem("prep_qk_ps"), sem("prep_v_ps")
        prep_qk, prep_v = sem("prep_qk"), sem("prep_v")
        m_ps, vw_ps = sem("m_ps"), sem("vw_ps")
        m_tmp, m_shift, m_hi, m_lo = sem("m_tmp"), sem("m_shift"), sem("m_hi"), sem("m_lo")
        vw_hi, vw_lo = sem("vw_hi"), sem("vw_lo")
        pool_passed, dve_passed = sem("pool_passed"), sem("dve_passed")
        ln_bn, ln_agg, ln_ve, ln_mean, ln_rstd, ln_keep = (sem("ln_bn"), sem("ln_agg"), sem("ln_ve"),
                                                           sem("ln_mean"), sem("ln_rstd"), sem("ln_keep"))
        ln_xn, ln_T = sem("ln_xn"), sem("ln_T")
        raw_T, logit_ps, logits_kept = sem("raw_T"), sem("logit_ps"), sem("logits_kept")
        route = [sem(f"route{r}") for r in range(2)]
        onehot_ready = [sem(f"onehot_ready{r}") for r in range(2)]
        rank_ps = [sem(f"rank_ps{r}") for r in range(2)]
        routed = [sem(f"routed{r}") for r in range(2)]
        sorted_rows = [sem(f"sorted_rows{r}") for r in range(2)]
        bias_in = [sem(f"bias_in{r}") for r in range(2)]
        bias_half = [sem(f"bias_half{r}") for r in range(2)]
        slot_in = [[sem(f"slot_in{r}_{k}") for k in range(NX)] for r in range(2)]
        slot_out = [[sem(f"slot_out{r}_{k}") for k in range(NX)] for r in range(2)]
        s_xn, s_xT, s_xhi, s_xlo, s_h, s_hb, s_hT, s_hhi, s_hlo, s_y, s_xb, s_yb, s_fin, s_ids = (
            [sem(f"{n}{r}") for r in range(2)] for n in
            ("slot_xn_ready", "slot_xT_ps", "slot_xT_hi_ready", "slot_xT_lo_ready", "h_ps", "h_ready", "hT_ps",
             "hT_hi_ready", "hT_lo_ready", "y_ps", "xb_ready", "y_half", "slot_done", "ids_kept"))
        x1_in = [sem("x1_first"), sem("x1_rest")]
        xT_hi, xT_lo = sem("xT_hi_ready"), sem("xT_lo_ready")
        scores, neg_max, probs, row_inv, normed = (sem("scores"), sem("neg_max_ready"), sem("probs_ready"),
                                                   sem("row_inv_ready"), sem("probs_normed"))
        pT_ps, pT_hi, pT_lo, av = sem("probsT_ps"), sem("probsT_hi_ready"), sem("probsT_lo_ready"), sem("av_done")
        o_kept, oT_ps, x2_ready = sem("o_kept"), sem("oT_ps"), sem("x2_ready")

        block = ctx.enter_context(nc.Block())

        HG = H * G
        BODY = 2 * HG
        UNITS = NG * HG
        LAG_T, LAG_AV = 2, 7

        def looped(it):
            return not isinstance(it, int)

        def rounds(eng, slot):
            for n in range(BODY + LAG_AV):
                slot(n, 0)
            with eng.Fori(1, NG // 2) as it:
                for n in range(LAG_AV, BODY + LAG_AV):
                    slot(n, it)

        def job_at(n, s):
            return n // HG if n % HG == s else None

        L_FIRST = NG

        def job_L(g, it):
            return (L_FIRST + 2 * g - 1 if isinstance(g, int) and g else L_FIRST) + 4 * it

        def job_E(g, it):
            return L_FIRST + 2 + 2 * g + 4 * it

        def tiles(eng, step, lags):
            full = (SLOTS - NX) // NX
            for m in range(NX):
                step(m, 0)
            with eng.Fori(0, full) as it:
                for m in range(NX, 2 * NX):
                    step(m, it)
            for m in range(NX * (full + 1), SLOTS + lags):
                step(m, 0)

        def live(m, lag):
            return 0 <= m - lag < SLOTS

        def tile_ap(ap2, m, it):
            return ap2[:, ds(m + NX * it, 1), :] if not isinstance(it, int) else ap2[:, m:m + 1, :]

        def expert(eng, j, it):
            at = ET[0:1, j:j + 1] if isinstance(it, int) else ET[0:1, ds(j + NX * it, 1)]
            return eng.value_load(at, min_val=0, max_val=E - 1)

        def apart(eng, passed):
            eng.sem_inc(passed, 1)

        @block.sync
        def _(sp):
            sp.dma_start(ROWS[:, :, 0:D], x_rows).then_inc(x_in, 16)
            sp.dma_start(GWR[:, :], gate_w).then_inc(small_in, 16)
            sp.dma_start(GB[:, :], gate_b.partition_broadcast(P)).then_inc(small_in, 16)
            sp.dma_start(EB[:, :], expert_bias.partition_broadcast(P)).then_inc(small_in, 16)
            sp.dma_start(BO[:, :], bout.rearrange("(d a) -> d a", a=1)).then_inc(small_in, 16)
            sp.dma_start(WRAW[:, :].rearrange("p (e f) -> p e f", e=E),
                         w1.rearrange("e d f -> d e f")).then_inc(w1_in, 16)
            sp.dma_start(CTX[:, :, :], context.rearrange("b m c -> (b m) c").rearrange("(k p) c -> p k c", p=P))\
                .then_inc(attw_in, 16)
            sp.dma_start(WQR[:, :, :], Wq.rearrange("d (h q) -> d h q", h=H)).then_inc(attw_in, 16)
            sp.dma_start(WKR[:, :, :], Wk.rearrange("c (h q) -> c h q", h=H)).then_inc(attw_in, 16)
            sp.dma_start(WVR[:, :, :], Wv.rearrange("c (h q) -> c h q", h=H)).then_inc(attw_in, 16)
            sp.dma_start(WOR[:, :, :], Wout.rearrange("(h p) q -> p h q", h=H)).then_inc(attw_in, 16)
            sp.wait_ge(w_lo, 1)
            for e in range(E):
                sp.dma_start(WRAW[:, e * F:(e + 1) * F].rearrange("p (c d) -> p c d", c=FC),
                             w2[e].rearrange("(c p) d -> p c d", p=P)).then_inc(w2_in, 16)

            def experts(r):
                if r == 0:
                    sp.wait_ge(w_lo, 2)
                    sp.wait_ge(m_lo, H)
                    sp.wait_ge(vw_lo, H)
                    sp.wait_ge(prep_v, H)
                else:
                    sp.wait_ge(av, UNITS)
                    sp.wait_ge(logits_kept, 2 * NG)
                sp.dma_start(B1[:, :, :], b1.partition_broadcast(P)).then_inc(bias_in[r], 16)
                sp.dma_start(B2[:, :, :], b2.partition_broadcast(P)).then_inc(bias_in[r], 16)
                sp.wait_ge(sorted_rows[r], 16 * T)

                slot_tiles = slots[r].rearrange("(j p) w -> p j w", p=P)

                def load(m, it):
                    if not live(m, 0):
                        return
                    if m >= NX:
                        sp.wait_ge(s_xb[r], m - NX + 1 + NX * it)
                        sp.wait_ge(s_ids[r], m - NX + 1 + NX * it)
                    sp.dma_start(XS[:, m % NX:m % NX + 1, :], tile_ap(slot_tiles, m, it))\
                        .then_inc(slot_in[r][m % NX], 16)

                tiles(sp, load, 0)

            experts(0)
            for k in range(NX):
                sp.wait_ge(slot_out[0][k], 16 * ((SLOTS - 1 - k) // NX + 1))
            sp.dma_start(ROWS[:, 0:G, 0:D], x1_rows[:, 0:G, :]).then_inc(x1_in[0], 16)
            sp.dma_start(ROWS[:, G:T, 0:D], x1_rows[:, G:T, :]).then_inc(x1_in[1], 16)
            experts(1)
            for k in range(NX):
                sp.wait_ge(slot_out[1][k], 16 * ((SLOTS - 1 - k) // NX + 1))

        @block.gpsimd
        def _(pool):
            pool.memset(IDN[:, :], 0.0).then_inc(zeroed, 1)
            pool.memset(BEFORE[:, :], 0.0).then_inc(zeroed, 1)
            pool.memset(FILL[:, :], 0.0).then_inc(zeroed, 1)
            pool.memset(ONES[:, :], 1.0)
            pool.memset(NHALF[:, :], -0.5)
            pool.memset(ONF[:, :], 1.0)
            pool.wait_ge(zeroed, 3)
            pool.affine_select(out=IDN[:, :], in_=IDN[:, :], compare_op=ALU.not_equal, fill=1.0, base=0,
                               pattern=[[-1, P]], channel_multiplier=1)
            pool.affine_select(out=BEFORE[:, :], in_=BEFORE[:, :], compare_op=ALU.is_ge, fill=1.0, base=0,
                               pattern=[[-1, P]], channel_multiplier=1)
            pool.iota(PREF[:, :], pattern=[[-1, E]], base=E, channel_multiplier=0,
                      allow_small_or_imprecise_dtypes=True)
            pool.iota(TIDX[:, :], pattern=[[1, SLOTS]], base=0, channel_multiplier=0,
                      allow_small_or_imprecise_dtypes=True).then_inc(consts_ready, 1)
            pool.iota(FILL[:, ID:ID + 1].bitcast(i32), pattern=[[0, 1]], base=N, channel_multiplier=0)\
                .then_inc(fill_ready, 1)
            pool.iota(ROWS[:, :, ID].bitcast(i32), pattern=[[1, T]], base=0, channel_multiplier=T)\
                .then_inc(consts_ready, 1)

            def rstd(job):
                pool.wait_ge(ln_ve, job + 1)
                pool.tensor_tensor(RS[:, :], VE[:, :], NHALF[:, :], ALU.pow).then_inc(ln_rstd, 1)

            with pool.Fori(0, NG) as g:
                rstd(g)

            def sort_rows(r):
                pool.wait_ge(slots_filled, 32)
                pool.wait_ge(routed[r], 1)
                pool.wait_ge(ln_keep, (NG, L_FIRST + 2 * NG + 1)[r])
                for t in range(T):
                    pool.indirect_dma_start(slots[r][:, :],
                                            bass.IndirectOffsetOnAxis(ap=POS[:, t:t + 1], axis=0),
                                            ROWS[:, t, :], None).then_inc(sorted_rows[r], 16)

            def experts(r):
                pool.wait_ge(bias_half[r], 1)

                def step(m, it):
                    if live(m, 2):
                        j = m - 2
                        e = expert(pool, j, it)
                        pool.wait_ge(slot_in[r][j % NX], 16 * (j // NX + 1) + 16 * it)
                        if j >= 2:
                            pool.wait_ge(s_yb[r], j - 1 + NX * it)
                        pool.tensor_tensor(XB[:, j % 2, :].unsqueeze(1), XS[:, j % NX, 0:D].unsqueeze(1),
                                           B2[:, ds(e, 1), :], ALU.add).then_inc(s_xb[r], 1)
                    if live(m, 4):
                        j = m - 4
                        pool.wait_ge(s_fin[r], j + 1 + NX * it)
                        apart(pool, pool_passed)
                        pool.indirect_dma_start(
                            ffn_dst[r], bass.IndirectOffsetOnAxis(ap=IDS[:, j % NX:j % NX + 1], axis=0),
                            RES[:, j % NX, :], None, bounds_check=N - 1, oob_is_err=False)\
                            .then_inc(slot_out[r][j % NX], 16)

                tiles(pool, step, 4)

            sort_rows(0)
            experts(0)
            rstd(L_FIRST)

            def slot(n, it):
                pool.wait_ge(row_inv, n + 1 + BODY * it)
                apart(pool, pool_passed)
                pool.tensor_scalar(PR[:, n % 4, :], PR[:, n % 4, :], RI[:, n % 4:n % 4 + 1], 1.0,
                                   ALU.mult, ALU.mult).then_inc(normed, 1)
                g = job_at(n, 11)
                if g is not None and (g >= 1 or looped(it)):
                    rstd(job_E(g - 1, it))
                g = job_at(n, 20)
                if g is not None:
                    rstd(job_L(g + 1, it))

            rounds(pool, slot)
            rstd(job_E(NG - 1, 0))
            sort_rows(1)
            experts(1)

        @block.scalar
        def _(act):
            act.wait_ge(fill_ready, 1)
            for r in range(2):
                act.dma_start(slots[r].rearrange("(j p) w -> p j w", p=P),
                              FILL[:, :].unsqueeze(1).to_broadcast([P, SLOTS, ROW])).then_inc(slots_filled, 16)
            act.wait_ge(w1_in, 16)
            act.activation(W1H[:, :, :].rearrange("p e f -> p (e f)"), WRAW[:, :], ACT.Copy).then_inc(w_hi, 1)

            def raw_evac(job, count):
                act.wait_ge(ln_T, job + 1)
                if looped(count) or count:
                    act.wait_ge(logit_ps, count)
                act.activation(XNT[:, :], BK[6][:, :], ACT.Copy).then_inc(raw_T, 1)

            raw_evac(0, 0)
            with act.Fori(1, NG) as g:
                raw_evac(g, g)

            act.wait_ge(ctxT_ps, 1)
            act.activation(CTXT[:, :], BK[0][0:C, :], ACT.Copy).then_inc(ctxT_ready, 1)

            def qk(h):
                act.wait_ge(prep_qk_ps, h + 1)
                if h:
                    act.wait_ge(m_ps, h)
                act.activation(WQT[:, :], BK[0][:, 0:P], ACT.Copy)
                act.activation(KT[:, :], BK[1][:, :], ACT.Copy).then_inc(prep_qk, 1)

            def products(h):
                act.wait_ge(m_ps, h + 1)
                if h:
                    act.wait_ge(m_lo, h)
                act.activation(MT[:, :], BK[3][:, :], ACT.Copy, scale=SHARPEN * SCALE, accum_out=SM[:, 0:1])\
                    .then_inc(m_tmp, 1)
                act.wait_ge(vw_ps, h + 1)
                act.activation(VWH[:, h, :, :].rearrange("p c d -> p (c d)"), BK[4][:, :], ACT.Copy)\
                    .then_inc(vw_hi, 1)

            for h in range(H):
                qk(h)
                products(h)
            act.wait_ge(w2_in, 16 * E)
            for c in range(2):
                eh = E // 2
                last = act.activation(
                    W2HL[:, c * eh:(c + 1) * eh, :, 0, :].rearrange("p e c d -> p (e c) d"),
                    WRAW[:, c * eh * F:(c + 1) * eh * F].rearrange("p (a d) -> p a d", d=D), ACT.Copy)
            last.then_inc(w_hi, 1)

            def experts(r):
                def step(m, it):
                    if live(m, 0):
                        act.wait_ge(s_xT[r], m + 1 + NX * it)
                        if m >= 2:
                            act.wait_ge(s_h[r], m - 1 + NX * it)
                        act.activation(XTH[:, m % 2, :], BK[m % 2][:, 0:P], ACT.Copy).then_inc(s_xhi[r], 1)
                    if live(m, 2):
                        j = m - 2
                        act.wait_ge(s_hT[r], j + 1 + NX * it)
                        if j >= 2:
                            act.wait_ge(s_y[r], j - 1 + NX * it)
                        act.activation(HTH[:, j % 2, :], BK[4 + j % 2][:, :], ACT.Relu).then_inc(s_hhi[r], 1)

                tiles(act, step, 2)

            experts(0)

            def xT_evac(g, it):
                act.wait_ge(ln_T, job_L(g, it) + 1)
                act.activation(AXH[:, g % 2, :], BK[6][:, :], ACT.Copy).then_inc(xT_hi, 1)

            xT_evac(0, 0)

            def slot(n, it):
                if n >= LAG_T:
                    u = n - LAG_T
                    act.wait_ge(pT_ps, u + 1 + BODY * it)
                    if u % G == 0 and (u // G >= 2 or looped(it)):
                        act.wait_ge(av, G * (u // G) - G + BODY * it)
                    act.activation(PTH[:, (u // G) % 2, :, (u % G) * P:(u % G + 1) * P],
                                   BK[2 + u % 2][:, :].rearrange("p (c q) -> p c q", c=KC), ACT.Copy)\
                        .then_inc(pT_hi, 1)
                act.wait_ge(neg_max, n + 1 + BODY * it)
                if n >= 4:
                    act.wait_ge(pT_ps, n - 3 + BODY * it)
                act.activation(PR[:, n % 4, :], BK[n % 2][:, :], ACT.Exp, bias=NM[:, n % 4:n % 4 + 1],
                               accum_out=SU[:, n % 4:n % 4 + 1]).then_inc(probs, 1)
                g = job_at(n, 7)
                if g is not None and (g >= 1 or looped(it)):
                    o_evac(g - 1, it)
                g = job_at(n, 15)
                if g is not None and (g >= 1 or looped(it)):
                    raw_evac(job_E(g - 1, it), NG + g - 1 + 2 * it)
                g = job_at(n, 24)
                if g is not None:
                    xT_evac(g + 1, it)

            def o_evac(g, it):
                act.wait_ge(av, HG * (g + 1) + BODY * it)
                if g >= 1 or looped(it):
                    act.wait_ge(oT_ps, g + 2 * it)
                act.activation(OT[:, :], BK[4 + g % 2][:, :], ACT.Identity, bias=BO[:, 0:1]).then_inc(o_kept, 1)

            rounds(act, slot)
            o_evac(NG - 1, 0)
            raw_evac(job_E(NG - 1, 0), 2 * NG - 1)
            experts(1)

        @block.vector
        def _(dve):
            v = nc.vector

            def stats(job, t0):
                apart(dve, dve_passed)
                for i in range(G):
                    t = t0 + i
                    row = ROWS[:, t, 0:D] if isinstance(t, int) else ROWS[:, ds(t, 1), 0:D].rearrange("p a d -> p (a d)")
                    last = v.bn_stats(BN[:, i, :], row)
                last.then_inc(ln_bn, 1)
                dve.wait_ge(ln_bn, job + 1)
                if looped(job) or job:
                    dve.wait_ge(ln_keep, job)
                apart(dve, dve_passed)
                for i in range(G):
                    last = v.bn_aggr(MV[:, i, :], BN[:, i, :])
                last.then_inc(ln_agg, 1)
                dve.wait_ge(ln_agg, job + 1)
                v.tensor_scalar(VE[:, :], MV[:, :, 1], EPS, None, ALU.add).then_inc(ln_ve, 1)

            def norm(job, t0, before):
                dve.wait_ge(ln_rstd, job + 1)
                if looped(job) or job:
                    dve.wait_ge(ln_T, job)
                for i in range(G):
                    t = t0 + i
                    row = ROWS[:, t, 0:D] if isinstance(t, int) else ROWS[:, ds(t, 1), 0:D].rearrange("p a d -> p (a d)")
                    last = v.tensor_scalar(XN[:, i, :], row, MV[:, i, 0:1], RS[:, i:i + 1], ALU.subtract, ALU.mult)
                last.then_inc(ln_xn, 1)
                span = ROWS[:, t0:t0 + G, :] if isinstance(t0, int) else ROWS[:, ds(t0, G), :]
                v.tensor_copy(span[:, :, MEAN:MEAN + 1], MV[:, :, 0:1])
                v.tensor_copy(span[:, :, RSTD:RSTD + 1], RS[:, :].unsqueeze(2)).then_inc(ln_keep, 1)

            def keep_logits(count, t0):
                dve.wait_ge(logit_ps, count)
                span = LG[:, t0:t0 + G, :] if isinstance(t0, int) else LG[:, ds(t0, G), :]
                v.tensor_copy(span, BK[7][:, 0:G * E].rearrange("p (t e) -> p t e", e=E)).then_inc(logits_kept, 1)

            def route_rows(r):
                step = [0]

                def link(ins):
                    step[0] += 1
                    ins.then_inc(route[r], 1)
                    dve.wait_ge(route[r], step[0])

                dve.wait_ge(logits_kept, NG * (r + 1))
                bias = lambda b: b[:, :].unsqueeze(1).to_broadcast([P, T, E])
                link(v.tensor_tensor(LG[:, :, :], LG[:, :, :], bias(GB), ALU.add))
                link(v.tensor_tensor(LG[:, :, :], LG[:, :, :], bias(EB), ALU.add))
                link(v.tensor_reduce(MX[:, :], LG[:, :, :], AX.X, ALU.max))
                link(v.tensor_tensor(LG[:, :, :], LG[:, :, :], MX[:, :].unsqueeze(2).to_broadcast([P, T, E]), ALU.is_ge))
                link(v.tensor_tensor(LG[:, :, :], LG[:, :, :], bias(PREF), ALU.mult))
                link(v.tensor_reduce(MX[:, :], LG[:, :, :], AX.X, ALU.max))
                v.tensor_tensor(OH[:, :, :].rearrange("p e t -> p t e"), LG[:, :, :],
                                MX[:, :].unsqueeze(2).to_broadcast([P, T, E]), ALU.is_equal)\
                    .then_inc(onehot_ready[r], 1)
                dve.wait_ge(rank_ps[r], 1)
                flat = lambda a: a[:, :, :].rearrange("p e t -> p (e t)")
                rank, total = BK[7][:, 0:E * T], BK[7][:, E * T:2 * E * T]
                c = lambda i: CNT[:, i, :]
                link(v.tensor_tensor_scan(flat(WRK), ONF[:, :], total, 0.0, ALU.mult, ALU.add))
                link(v.tensor_copy(c(0), WRK[:, :, T - 1]))
                v.tensor_copy(CNT[:, 1, 0:1], CNT[:, 0, 0:1])
                link(v.tensor_tensor(CNT[:, 1, 1:E], CNT[:, 0, 1:E], CNT[:, 0, 0:E - 1], ALU.subtract))
                link(v.tensor_scalar(CNTI[:, 0, :], c(1), float(P - 1), None, ALU.add))
                link(v.tensor_scalar(CNTI[:, 1, :], CNTI[:, 0, :], 7, None, ALU.arith_shift_right))
                link(v.tensor_copy(c(2), CNTI[:, 1, :]))
                link(v.tensor_tensor_scan(c(3), ONF[:, 0:E], c(2), 0.0, ALU.mult, ALU.add))
                link(v.tensor_tensor(c(4), c(3), c(2), ALU.subtract))
                link(v.tensor_scalar(c(4), c(4), float(P), None, ALU.mult))
                link(v.tensor_tensor(c(5), c(0), c(1), ALU.subtract))
                link(v.tensor_tensor(c(4), c(4), c(5), ALU.subtract))
                link(v.tensor_tensor(flat(WRK), flat(WRK), total, ALU.subtract))
                link(v.tensor_tensor(flat(WRK), flat(WRK), rank, ALU.add))
                link(v.tensor_tensor(WRK[:, :, :], WRK[:, :, :], c(4).unsqueeze(2).to_broadcast([P, E, T]), ALU.add))
                link(v.tensor_tensor(WRK[:, :, :], WRK[:, :, :], OH[:, :, :], ALU.mult))
                link(v.tensor_reduce(MX[:, :], WRK[:, :, :].rearrange("p e t -> p t e"), AX.X, ALU.add))
                link(v.tensor_copy(POS[:, :], MX[:, :]))
                link(v.tensor_tensor(SEL[:, :, :], CNT[:, 3, 0:E - 1].unsqueeze(1).to_broadcast([P, SLOTS, E - 1]),
                                     TIDX[:, :].unsqueeze(2).to_broadcast([P, SLOTS, E - 1]), ALU.is_le))
                link(v.tensor_reduce(ETF[:, :], SEL[:, :, :], AX.X, ALU.add))
                v.tensor_copy(ET[:, :], ETF[:, :]).then_inc(routed[r], 1)

            def split_w1():
                dve.wait_ge(w_hi, 1)
                flat = lambda a: a[:, :, :].rearrange("p e f -> p (e f)")
                v.tensor_tensor(flat(W1L), WRAW[:, :], flat(W1H).bitcast(fp32), ALU.subtract).then_inc(w_lo, 1)

            def experts(r):
                dve.wait_ge(bias_in[r], 32)
                v.tensor_scalar(B2[:, :, :], B2[:, :, :], 0.5, None, ALU.mult).then_inc(bias_half[r], 1)

                def slot_norm(m, it):
                    dve.wait_ge(slot_in[r][m % NX], 16 * (m // NX + 1) + 16 * it)
                    if m >= 2:
                        dve.wait_ge(s_xT[r], m - 1 + NX * it)
                    v.tensor_scalar(XSN[:, m % 2, :], XS[:, m % NX, 0:D], XS[:, m % NX, MEAN:MEAN + 1],
                                    XS[:, m % NX, RSTD:RSTD + 1], ALU.subtract, ALU.mult).then_inc(s_xn[r], 1)
                    if m >= NX:
                        dve.wait_ge(slot_out[r][m % NX], 16 * (m // NX) + 16 * it)
                    v.tensor_copy(IDS[:, m % NX:m % NX + 1], XS[:, m % NX, ID:ID + 1].bitcast(i32))\
                        .then_inc(s_ids[r], 1)

                def step(m, it):
                    if live(m, 0):
                        dve.wait_ge(s_xhi[r], m + 1 + NX * it)
                        v.tensor_tensor(XTL[:, m % 2, :], BK[m % 2][:, 0:P], XTH[:, m % 2, :].bitcast(fp32),
                                        ALU.subtract).then_inc(s_xlo[r], 1)
                    if live(m, 1):
                        j = m - 1
                        e = expert(dve, j, it)
                        dve.wait_ge(s_h[r], j + 1 + NX * it)
                        if j >= 2:
                            dve.wait_ge(s_hT[r], j - 1 + NX * it)
                        v.tensor_tensor(HB[:, j % 2, :].unsqueeze(1), BK[2 + j % 2][:, :].unsqueeze(1),
                                        B1[:, ds(e, 1), :], ALU.add).then_inc(s_hb[r], 1)
                    if live(m, 2):
                        j = m - 2
                        dve.wait_ge(s_hhi[r], j + 1 + NX * it)
                        v.scalar_tensor_tensor(out=HTL[:, j % 2, :], in0=BK[4 + j % 2][:, :], scalar=0.0,
                                               in1=HTH[:, j % 2, :].bitcast(fp32), op0=ALU.max,
                                               op1=ALU.subtract).then_inc(s_hlo[r], 1)
                    if live(m, -1):
                        slot_norm(m + 1, it)
                    if live(m, 4):
                        j = m - 4
                        dve.wait_ge(s_y[r], j + 1 + NX * it)
                        dve.wait_ge(s_xb[r], j + 1 + NX * it)
                        v.scalar_tensor_tensor(out=YT[:, j % 2, :], in0=BK[6 + j % 2][:, D:2 * D], scalar=0.5,
                                               in1=XB[:, j % 2, :], op0=ALU.mult, op1=ALU.add).then_inc(s_yb[r], 1)
                        dve.wait_ge(s_yb[r], j + 1 + NX * it)
                        v.scalar_tensor_tensor(out=RES[:, j % NX, :], in0=BK[6 + j % 2][:, 0:D], scalar=0.5,
                                               in1=YT[:, j % 2, :], op0=ALU.mult, op1=ALU.add).then_inc(s_fin[r], 1)

                slot_norm(0, 0)
                tiles(dve, step, 4)

            dve.wait_ge(x_in, 16)
            dve.wait_ge(consts_ready, 2)
            dve.wait_ge(small_in, 64)
            dve.wait_ge(gate_ps, 1)
            v.tensor_copy(GWT[:, :], BK[5][:, 0:E]).then_inc(gate_ready, 1)
            stats(0, 0)
            norm(0, 0, 0)
            with dve.Fori(1, NG) as g:
                stats(g, G * g)
                norm(g, G * g, g)
                keep_logits(g, G * g - G)
            keep_logits(NG, T - G)
            route_rows(0)
            split_w1()
            for h in range(H):
                dve.wait_ge(prep_v_ps, h + 1)
                if h:
                    dve.wait_ge(vw_ps, h)
                v.tensor_copy(VT[:, :], BK[2][:, :]).then_inc(prep_v, 1)
                dve.wait_ge(m_tmp, h + 1)
                v.tensor_scalar(SM[:, 1:2], SM[:, 0:1], -(SHARPEN - 1.0) / (SHARPEN * KEYS), None, ALU.mult)\
                    .then_inc(m_shift, 1)
                dve.wait_ge(m_shift, h + 1)
                v.tensor_scalar(MH[:, h, :], MT[:, :], SM[:, 1:2], None, ALU.add).then_inc(m_hi, 1)
                dve.wait_ge(m_hi, h + 1)
                v.scalar_tensor_tensor(out=ML[:, h, :], in0=MT[:, :], scalar=SM[:, 1:2],
                                       in1=MH[:, h, :].bitcast(fp32), op0=ALU.add, op1=ALU.subtract).then_inc(m_lo, 1)
                dve.wait_ge(vw_hi, h + 1)
                v.tensor_tensor(VWL[:, h, :, :].rearrange("p c d -> p (c d)"), BK[4][:, :],
                                VWH[:, h, :, :].rearrange("p c d -> p (c d)").bitcast(fp32), ALU.subtract)\
                    .then_inc(vw_lo, 1)
            dve.wait_ge(w_hi, 2)
            v.tensor_tensor(W2HL[:, :, :, 1, :].rearrange("p e c d -> p (e c) d"),
                            WRAW[:, :].rearrange("p (a d) -> p a d", d=D),
                            W2HL[:, :, :, 0, :].rearrange("p e c d -> p (e c) d").bitcast(fp32), ALU.subtract)\
                .then_inc(w_lo, 1)

            experts(0)

            def xT_low(g, it):
                dve.wait_ge(xT_hi, g + 1 + 2 * it)
                v.tensor_tensor(AXL[:, g % 2, :], BK[6][:, :], AXH[:, g % 2, :].bitcast(fp32), ALU.subtract)\
                    .then_inc(xT_lo, 1)

            dve.wait_ge(x1_in[0], 16)
            stats(L_FIRST, 0)
            norm(L_FIRST, 0, 0)
            xT_low(0, 0)

            def new_rows(g, it):
                dve.wait_ge(oT_ps, g + 1 + 2 * it)
                span = (ROWS[:, G * g:G * g + G, 0:D] if not looped(it) else ROWS[:, ds(G * g + 2 * G * it, G), 0:D])
                v.tensor_tensor(span, span, BK[7][:, :].rearrange("p (t d) -> p t d", d=D), ALU.add)\
                    .then_inc(x2_ready, 1)
                dve.wait_ge(x2_ready, g + 1 + 2 * it)

            def slot(n, it):
                dve.wait_ge(scores, n + 1 + BODY * it)
                v.tensor_reduce(NM[:, n % 4:n % 4 + 1], BK[n % 2][:, :], AX.X, ALU.max, negate=True)\
                    .then_inc(neg_max, 1)
                if n >= LAG_T:
                    u = n - LAG_T
                    dve.wait_ge(pT_hi, u + 1 + BODY * it)
                    at = (slice(None), (u // G) % 2, slice(None), slice((u % G) * P, (u % G + 1) * P))
                    v.tensor_tensor(PTL[at], BK[2 + u % 2][:, :].rearrange("p (c q) -> p c q", c=KC),
                                    PTH[at].bitcast(fp32), ALU.subtract).then_inc(pT_lo, 1)
                dve.wait_ge(probs, n + 1 + BODY * it)
                v.reciprocal(RI[:, n % 4:n % 4 + 1], SU[:, n % 4:n % 4 + 1]).then_inc(row_inv, 1)
                g = job_at(n, 10)
                if g is not None and (g >= 1 or looped(it)):
                    new_rows(g - 1, it)
                    stats(job_E(g - 1, it), G * (g - 1) + 2 * G * it)
                g = job_at(n, 12)
                if g is not None and (g >= 1 or looped(it)):
                    norm(job_E(g - 1, it), G * (g - 1) + 2 * G * it, 0)
                g = job_at(n, 18)
                if g is not None and (g >= 1 or looped(it)):
                    keep_logits(NG + g + 2 * it, G * (g - 1) + 2 * G * it)
                for s, work in ((19, stats), (21, lambda j, t: norm(j, t, 0))):
                    g = job_at(n, s)
                    if g is not None:
                        if n == s and not looped(it):
                            dve.wait_ge(x1_in[1], 16)
                        t0 = G * (g + 1) + 2 * G * it
                        work(job_L(g + 1, it), t0 if not looped(it) else (t0 % T))
                g = job_at(n, 25)
                if g is not None:
                    xT_low(g + 1, it)

            rounds(dve, slot)
            new_rows(NG - 1, 0)
            stats(job_E(NG - 1, 0), T - G)
            norm(job_E(NG - 1, 0), T - G, 0)
            keep_logits(2 * NG, T - G)
            route_rows(1)
            experts(1)

        @block.tensor
        def _(pe):
            def xn_transposes(job):
                pe.wait_ge(ln_xn, job + 1)
                for i in range(G):
                    last = pe.transpose(BK[6][:, i * P:(i + 1) * P], XN[:, i, :], IDN[:, :])
                last.then_inc(ln_T, 1)

            def gate_logits(count):
                pe.wait_ge(raw_T, count)
                for i in range(G):
                    last = pe.matmul(BK[7][:, i * E:(i + 1) * E], XNT[:, i * P:(i + 1) * P], GWT[:, :],
                                     start=True, stop=True)
                last.then_inc(logit_ps, 1)

            def ranks(r):
                pe.wait_ge(onehot_ready[r], 1)
                rhs = OH[:, :, :].rearrange("p e t -> p (e t)")
                pe.matmul(BK[7][:, 0:E * T], BEFORE[:, :], rhs, start=True, stop=True)
                pe.matmul(BK[7][:, E * T:2 * E * T], ONES[:, :], rhs, start=True, stop=True).then_inc(rank_ps[r], 1)

            def three(out, wh, wl, mh, ml, start, stop):
                pe.matmul(out, wh, mh, start=start, stop=False)
                pe.matmul(out, wh, ml, start=False, stop=False)
                return pe.matmul(out, wl, mh, start=False, stop=stop)

            def experts(r):
                def step(m, it):
                    if live(m, 0):
                        pe.wait_ge(s_xn[r], m + 1 + NX * it)
                        if m >= 2:
                            pe.wait_ge(s_xlo[r], m - 1 + NX * it)
                        pe.transpose(BK[m % 2][:, 0:P], XSN[:, m % 2, :], IDN[:, :]).then_inc(s_xT[r], 1)
                    if live(m, 1):
                        j = m - 1
                        e = expert(pe, j, it)
                        pe.wait_ge(s_xlo[r], j + 1 + NX * it)
                        if j >= 2:
                            pe.wait_ge(s_hb[r], j - 1 + NX * it)
                        three(BK[2 + j % 2][:, :].unsqueeze(1), XTH[:, j % 2, :], XTL[:, j % 2, :],
                              W1H[:, ds(e, 1), :], W1L[:, ds(e, 1), :], True, True).then_inc(s_h[r], 1)
                    if live(m, 2):
                        j = m - 2
                        pe.wait_ge(s_hb[r], j + 1 + NX * it)
                        if j >= 2:
                            pe.wait_ge(s_hlo[r], j - 1 + NX * it)
                        for c in range(FC):
                            last = pe.transpose(BK[4 + j % 2][:, c * P:(c + 1) * P], HB[:, j % 2, c * P:(c + 1) * P],
                                                IDN[:, :])
                        last.then_inc(s_hT[r], 1)
                    if live(m, 3):
                        j = m - 3
                        e = expert(pe, j, it)
                        pe.wait_ge(s_hlo[r], j + 1 + NX * it)
                        if j >= 2:
                            pe.wait_ge(s_fin[r], j - 1 + NX * it)
                        for c in range(FC):
                            pe.matmul(BK[6 + j % 2][:, 0:2 * D].rearrange("p (a s d) -> p a s d", a=1, s=2),
                                      HTH[:, j % 2, c * P:(c + 1) * P], W2HL[:, ds(e, 1), c, :, :],
                                      start=(c == 0), stop=False)
                            last = pe.matmul(BK[6 + j % 2][:, 0:D].unsqueeze(1), HTL[:, j % 2, c * P:(c + 1) * P],
                                             W2HL[:, ds(e, 1), c, 0, :], start=False, stop=(c == FC - 1))
                        last.then_inc(s_y[r], 1)

                tiles(pe, step, 3)

            pe.wait_ge(consts_ready, 2)
            pe.wait_ge(small_in, 64)
            pe.transpose(BK[5][:, 0:E], GWR[:, :], IDN[0:E, 0:E]).then_inc(gate_ps, 1)
            pe.wait_ge(gate_ready, 1)
            xn_transposes(0)
            with pe.Fori(1, NG) as g:
                gate_logits(g)
                pe.wait_ge(logits_kept, g)
                pe.wait_ge(raw_T, g)
                xn_transposes(g)
            gate_logits(NG)
            pe.wait_ge(logits_kept, NG)
            ranks(0)
            pe.wait_ge(attw_in, 16 * 5)
            for c in range(KC):
                last = pe.transpose(BK[0][0:C, c * P:(c + 1) * P], CTX[:, c, :], IDN[:, :])
            last.then_inc(ctxT_ps, 1)
            pe.wait_ge(ctxT_ready, 1)

            def head_inputs(h):
                if h:
                    pe.wait_ge(prep_qk, h)
                    pe.wait_ge(prep_v, h)
                pe.transpose(BK[0][:, 0:P], WQR[:, h, :], IDN[:, :])
                pe.matmul(BK[1][:, :], WKR[:, h, :], CTXT[:, :], start=True, stop=True).then_inc(prep_qk_ps, 1)
                pe.matmul(BK[2][:, :], WVR[:, h, :], CTXT[:, :], start=True, stop=True).then_inc(prep_v_ps, 1)

            def head_products(h):
                pe.wait_ge(prep_qk, h + 1)
                if h:
                    pe.wait_ge(m_tmp, h)
                    pe.wait_ge(vw_lo, h)
                pe.matmul(BK[3][:, :], WQT[:, :], KT[:, :], start=True, stop=True).then_inc(m_ps, 1)
                pe.wait_ge(prep_v, h + 1)
                for c in range(KC):
                    last = pe.matmul(BK[4][:, c * D:(c + 1) * D], VT[:, c * P:(c + 1) * P], WOR[:, h, :],
                                     start=True, stop=True)
                last.then_inc(vw_ps, 1)

            head_inputs(0)
            for h in range(H):
                head_products(h)
                if h < H - 1:
                    head_inputs(h + 1)

            pe.wait_ge(w_lo, 2)
            pe.wait_ge(vw_lo, H)
            pe.wait_ge(routed[0], 1)
            experts(0)

            pe.wait_ge(s_fin[0], SLOTS)
            xn_transposes(L_FIRST)

            def slot(n, it):
                g = n // HG
                u = n
                h = (u // G) % H
                i = u % G
                if u % HG == 0:
                    pe.wait_ge(xT_lo, g + 1 + 2 * it)
                if u >= 2:
                    pe.wait_ge(probs, u - 1 + BODY * it)
                cols = slice(i * P, (i + 1) * P)
                three(BK[u % 2][:, :], AXH[:, g % 2, cols], AXL[:, g % 2, cols], MH[:, h, :], ML[:, h, :],
                      True, True).then_inc(scores, 1)
                if n >= LAG_T:
                    u = n - LAG_T
                    pe.wait_ge(normed, u + 1 + BODY * it)
                    if u >= 2:
                        pe.wait_ge(pT_lo, u - 1 + BODY * it)
                    for c in range(KC):
                        last = pe.transpose(BK[2 + u % 2][:, c * P:(c + 1) * P], PR[:, u % 4, c * P:(c + 1) * P],
                                            IDN[:, :])
                    last.then_inc(pT_ps, 1)
                if n >= LAG_AV:
                    u = n - LAG_AV
                    g, h, c = u // HG, (u // G) % H, u % G
                    hh = u // G
                    if c == 0:
                        pe.wait_ge(pT_lo, G * hh + G + BODY * it)
                        if h == 0 and (g >= 2 or looped(it)):
                            pe.wait_ge(o_kept, g - 1 + 2 * it)
                    three(BK[4 + g % 2][:, :], VWH[:, h, c, :], VWL[:, h, c, :], PTH[:, hh % 2, c, :],
                          PTL[:, hh % 2, c, :], h == 0 and c == 0, h == H - 1 and c == KC - 1).then_inc(av, 1)
                g = job_at(n, 9)
                if g is not None and (g >= 1 or looped(it)):
                    o_transposes(g - 1, it)
                g = job_at(n, 14)
                if g is not None and (g >= 1 or looped(it)):
                    pe.wait_ge(xT_lo, g + 1 + 2 * it)
                    xn_transposes(job_E(g - 1, it))
                g = job_at(n, 17)
                if g is not None and (g >= 1 or looped(it)):
                    gate_logits(NG + g + 2 * it)
                g = job_at(n, 23)
                if g is not None:
                    pe.wait_ge(raw_T, NG + g + 2 * it)
                    xn_transposes(job_L(g + 1, it))

            def o_transposes(g, it):
                pe.wait_ge(o_kept, g + 1 + 2 * it)
                pe.wait_ge(logits_kept, NG + g + 2 * it)
                for i in range(G):
                    last = pe.transpose(BK[7][:, i * D:(i + 1) * D], OT[:, i * P:(i + 1) * P], IDN[:, :])
                last.then_inc(oT_ps, 1)

            rounds(pe, slot)
            o_transposes(NG - 1, 0)
            pe.wait_ge(xT_lo, NG + 1)
            xn_transposes(job_E(NG - 1, 0))
            pe.wait_ge(x2_ready, NG)
            gate_logits(2 * NG)
            pe.wait_ge(logits_kept, 2 * NG)
            ranks(1)
            pe.wait_ge(routed[1], 1)
            experts(1)


_INS = ["L0_attn_x", "L0_attn_context", "L0_attn_Wq", "L0_attn_Wk", "L0_attn_Wv", "L0_attn_Wout", "L0_attn_bout",
        "L0_ffn_gate_w", "L0_ffn_gate_b", "L0_ffn_expert_bias", "L0_ffn_w1", "L0_ffn_b1", "L0_ffn_w2", "L0_ffn_b2"]


def kernel(**inputs):
    import numpy as _np
    import concourse.bacc as _bacc
    from concourse import mybir as _mybir
    from concourse.bass_utils import run_bass_kernel_spmd as _run

    nc = _bacc.Bacc("TRN2", target_bir_lowering=False, num_devices=1)
    arrays, args = {}, []
    for name in _INS:
        a = _np.ascontiguousarray(inputs[name])
        arrays[f"in_{name}"] = a
        args.append(nc.dram_tensor(f"in_{name}", a.shape, _mybir.dt.from_np(a.dtype), kind="ExternalInput").ap())
    shape = tuple(inputs["L0_attn_x"].shape)
    out = nc.dram_tensor("out_0", shape, _mybir.dt.float32, kind="ExternalOutput").ap()
    macaron_kernel(nc, *args, out)
    r = _run(nc, [arrays], core_ids=[0])
    return r.results[0]["out_0"]
```

```python
import concourse.bass as bass
from concourse import mybir
from contextlib import ExitStack

P = 128
EPS = 1e-05


def macaron_kernel(nc, x, context, Wq, Wk, Wv, Wout, bout, gate_w, gate_b, expert_bias, w1, b1, w2, b2, out):
    fp32, f32r, i32, bf16 = (mybir.dt.float32, mybir.dt.float32r, mybir.dt.int32, mybir.dt.bfloat16)
    ALU = mybir.AluOpType
    ACT = mybir.ActivationFunctionType
    AX = mybir.AxisListType
    ds = bass.ds

    N = x.shape[0] * x.shape[1]
    D = x.shape[2]
    T = N // P
    KEYS = context.shape[0] * context.shape[1]
    KC = KEYS // P
    C = context.shape[2]
    H = Wq.shape[1] // D
    SCALE = float(D) ** -0.5
    SHARPEN = 1.5
    E, F = w1.shape[0], w1.shape[2]
    FC = F // P
    SLOTS = T + E - 1
    G = 4
    NG = T // G
    ROW = D + 3
    ID, SHIFT, RSTD = D, D + 1, D + 2

    x_rows = x.rearrange("b n d -> (b n) d").rearrange("(p t) d -> p t d", t=T)
    out_rows = out.rearrange("b n d -> (b n) d")
    x1 = nc.dram_tensor("x1", [N, D], fp32, kind="Internal").ap()
    REGION = T + 1
    EMPTY = SLOTS - T
    B1_EARLY = 3 * H * D // F
    slots = [nc.dram_tensor(f"slots{r}", [(E * REGION + EMPTY) * P, ROW], fp32, kind="Internal").ap()
             for r in range(2)]
    x1_rows = x1.rearrange("(p t) d -> p t d", t=T)
    ffn_dst = [x1, out_rows]

    ctx = ExitStack()
    with ctx:
        def sb(name, shape, dt, where=ctx):
            return where.enter_context(nc.sbuf_tensor(name, shape, dt))

        def sem(name):
            return ctx.enter_context(nc.semaphore(name))

        ROWS = sb("rows", [P, T, ROW], fp32)
        W1H = sb("w1_hi", [P, E, F], f32r)
        W1L = sb("w1_lo", [P, E, F], f32r)
        W2HL = sb("w2_hi_lo", [P, E, FC, 2, D], f32r)
        MH = sb("m_hi", [P, H, KEYS], f32r)
        ML = sb("m_lo", [P, H, KEYS], f32r)
        VWH = sb("vw_hi", [P, H, KC, D], f32r)
        VWL = sb("vw_lo", [P, H, KC, D], f32r)
        XN = sb("xn", [P, G, D], fp32)
        XNT = sb("xnT_or_oT", [P, G * P], fp32)
        X2 = [sb(f"x2_rows{k}", [P, G, ROW], fp32) for k in range(2)]
        IDN = sb("ident", [P, P], fp32)
        BEFORE = sb("before", [P, P], bf16)
        ONES = sb("ones", [P, P], bf16)
        FILL = sb("fill", [P, ROW], fp32)
        NHALF = sb("nhalf", [P, G], fp32)
        GWR = sb("gate_w", [E, D], fp32)
        GWT = sb("gate_wT", [P, E], fp32)
        GB = sb("gate_b", [P, E], fp32)
        EB = sb("expert_bias", [P, E], fp32)
        BO = sb("bout", [P, 1], fp32)
        PREF = sb("pref", [P, E], fp32)
        TIDX = sb("tile_index", [P, SLOTS], fp32)
        BN = [sb(f"bn{k}", [P, G, 6], fp32) for k in range(2)]
        MV = [sb(f"mean_var{k}", [P, G, 2], fp32) for k in range(2)]
        VE = [sb(f"var_eps{k}", [P, G], fp32) for k in range(2)]
        RS = [sb(f"rstd{k}", [P, G], fp32) for k in range(2)]
        SH = [sb(f"shift{k}", [P, G], fp32) for k in range(2)]
        LG = sb("logits", [P, G, E], fp32)
        MX = sb("row_max", [P, G], fp32)
        OH = [[sb(f"onehot{r}_{k}", [P, E, 1 + G], bf16) for k in range(2)] for r in range(2)]
        BASE = sb("region_base", [P, E, G], bf16)
        BASER = sb("region_row", [P, E], fp32)
        WRK = sb("route_work", [P, E, G], fp32)
        POSF = sb("pos_f", [P, G], fp32)
        POS = [sb(f"pos{k}", [P, G], i32) for k in range(2)]
        CNT = sb("counts", [P, 3, E], fp32)
        CNTI = sb("counts_int", [P, 2, E], i32)
        TAIL = sb("region_tail", [P, E], i32)
        ET = sb("expert_of_tile", [P, SLOTS], i32)
        TB = sb("block_of_tile", [P, SLOTS], i32)
        ETF = sb("tile_f", [P, SLOTS], fp32)
        SEL = sb("sel", [P, SLOTS, E], fp32)
        ONF = sb("ones_f", [P, 1], fp32)

        with ExitStack() as prep:
            WQR = sb("wq", [P, H, D], fp32, prep)
            WKR = sb("wk", [C, H, D], fp32, prep)
            WVR = sb("wv", [C, H, D], fp32, prep)
            WOR = sb("wout", [P, H, D], fp32, prep)
            CTX = sb("ctx", [P, KC, C], fp32, prep)
            CTXT = sb("ctxT", [C, KEYS], fp32, prep)
            WQT = sb("wqT", [P, P], fp32, prep)
            KT = sb("kT", [P, KEYS], fp32, prep)
            VT = sb("vT", [P, KEYS], fp32, prep)
            MT = sb("m_tmp", [P, KEYS], fp32, prep)
            SM = sb("m_sum", [P, 2], fp32, prep)
            WRAW = sb("w_raw", [P, E, F], fp32, prep)
        with ExitStack() as ffn:
            B1 = sb("b1", [P, E, F], fp32, ffn)
            B2 = sb("b2", [P, E, D], fp32, ffn)
            NX = 6
            XS = sb("slot_rows", [P, NX, ROW], fp32, ffn)
            RES = sb("result_rows", [P, NX, D], fp32, ffn)
            IDS = sb("result_ids", [P, NX], i32, ffn)
            XSN = sb("slot_xn", [P, 2, D], fp32, ffn)
            XTH = sb("slot_xT_hi", [P, 2, P], f32r, ffn)
            XTL = sb("slot_xT_lo", [P, 2, P], f32r, ffn)
            HB = sb("h", [P, 3, F], fp32, ffn)
            HTH = sb("hT_hi", [P, 2, FC * P], f32r, ffn)
            HTL = sb("hT_lo", [P, 2, FC * P], f32r, ffn)
            XB = sb("x_b2", [P, NX, D], fp32, ffn)
            XB2 = sb("x_b2_y", [P, 2, D], fp32, ffn)
            YT = sb("y_lo_half", [P, 2, D], fp32, ffn)
        with ExitStack() as att:
            PTH = sb("probsT_hi", [P, 2, KC, G * P], f32r, att)
            PTL = sb("probsT_lo", [P, 2, KC, G * P], f32r, att)
            PR = sb("probs", [P, 4, KEYS], fp32, att)
            AXH = sb("xT_hi", [P, 2, G * P], f32r, att)
            AXL = sb("xT_lo", [P, 2, G * P], f32r, att)
            NM = sb("neg_max", [P, 4], fp32, att)
            SU = sb("row_sum", [P, 4], fp32, att)
            RI = sb("row_inv", [P, 4], fp32, att)

        BK = [ctx.enter_context(nc.psum_tensor(f"bank{i}", [P, 512], fp32)) for i in range(8)]

        x_in = [sem(f"x_in{k}") for k in range(3)]
        small_in = sem("small_in")
        w1_in = [sem(f"w1_in{k}") for k in range(2)]
        w2_in = [sem(f"w2_in{e}") for e in range(E)]
        attw_in = sem("attw_in")
        slots_filled = sem("slots_filled")
        memsets = sem("memsets")
        consts_ready = sem("consts_ready")
        fill_ready = sem("fill_ready")
        gate_ps, gate_ready = sem("gate_ps"), sem("gate_ready")
        w1_hi, w1_lo, w2_hi, w2_lo = sem("w1_hi"), sem("w1_lo"), sem("w2_hi"), sem("w2_lo")
        ctxT_ps, ctxT_ready = sem("ctxT_ps"), sem("ctxT_ready")
        prep_qk_ps, prep_v_ps = sem("prep_qk_ps"), sem("prep_v_ps")
        prep_qk, prep_v = sem("prep_qk"), sem("prep_v")
        m_ps, vw_ps = sem("m_ps"), sem("vw_ps")
        m_tmp, m_shift, m_hi, m_lo = sem("m_tmp"), sem("m_shift"), sem("m_hi"), sem("m_lo")
        vw_hi, vw_lo = sem("vw_hi"), sem("vw_lo")
        pool_passed, dve_passed = sem("pool_passed"), sem("dve_passed")
        ln_bn, ln_agg, ln_ve, ln_rstd, ln_shift, ln_xn, ln_T = (
            [sem(f"{n}{k}") for k in range(2)] for n in ("ln_bn", "ln_agg", "ln_ve", "ln_rstd", "ln_shift", "ln_xn", "ln_T"))
        ln_keep = sem("ln_keep")
        raw_T, logit_ps = sem("raw_T"), sem("logit_ps")
        onehot_step, onehot_ready, sum_ready = sem("onehot_step"), sem("onehot_ready"), sem("sum_ready")
        rank_ps, ranked, pos_step, pos_ready = sem("rank_ps"), sem("ranked"), sem("pos_step"), sem("pos_ready")
        sorted_rows = [sem(f"sorted_rows{k}") for k in range(2)]
        total_ps = [sem(f"total_ps{r}") for r in range(2)]
        table_step = [sem(f"table_step{r}") for r in range(2)]
        tail_ready = [sem(f"tail_ready{r}") for r in range(2)]
        tail_filled = [sem(f"tail_filled{r}") for r in range(2)]
        routed = [sem(f"routed{r}") for r in range(2)]
        b1_in = [sem(f"b1_in{r}") for r in range(2)]
        b2_in = [sem(f"b2_in{r}") for r in range(2)]
        bias_half = [sem(f"bias_half{r}") for r in range(2)]
        slot_in = [[sem(f"slot_in{r}_{k}") for k in range(NX)] for r in range(2)]
        slot_out = [[sem(f"slot_out{r}_{k}") for k in range(NX)] for r in range(2)]
        s_xn, s_xT, s_xhi, s_xlo, s_h, s_hb, s_hT, s_hhi, s_hlo, s_y, s_xb, s_yb, s_fin, s_ids, s_x2 = (
            [sem(f"{n}{r}") for r in range(2)] for n in
            ("slot_xn_ready", "slot_xT_ps", "slot_xT_hi_ready", "slot_xT_lo_ready", "h_ps", "h_ready", "hT_ps",
             "hT_hi_ready", "hT_lo_ready", "y_ps", "y_hi_added", "y_lo_half", "slot_done", "ids_kept", "x_b2_ready"))
        x1_in = [sem("x1_first"), sem("x1_rest")]
        xT_hi, xT_lo = sem("xT_hi_ready"), sem("xT_lo_ready")
        scores, neg_max, probs, row_inv, normed = (sem("scores"), sem("neg_max_ready"), sem("probs_ready"),
                                                   sem("row_inv_ready"), sem("probs_normed"))
        pT_ps, pT_hi, pT_lo, av = sem("probsT_ps"), sem("probsT_hi_ready"), sem("probsT_lo_ready"), sem("av_done")
        o_kept, oT_ps, x2_ready = sem("o_kept"), sem("oT_ps"), sem("x2_ready")

        block = ctx.enter_context(nc.Block())

        HG = H * G
        BODY = 2 * HG
        UNITS = NG * HG
        LAG_T, LAG_AV = 3, 8

        def looped(it):
            return not isinstance(it, int)

        def rounds(eng, slot):
            for n in range(BODY + LAG_AV):
                slot(n, 0)
            with eng.Fori(1, NG // 2) as it:
                for n in range(LAG_AV, BODY + LAG_AV):
                    slot(n, it)

        def at_step(n, it, s, back=0):
            return [n // HG] if n % HG == s and (n // HG >= back or looped(it)) else []

        def group_tile(g, it):
            return (G * g + 2 * G * it) % T if looped(it) else G * g

        GATE, ATT = 0, 1
        RANKS, TOTALS = 0, 64
        RANK_BANK = [5, 7]

        def shifted(g, it, k=2):
            return g + k * it if looped(it) else g

        def tiles(eng, step, lags):
            full = (SLOTS - NX) // NX
            for m in range(2 * NX):
                step(m, 0)
            with eng.Fori(1, full) as it:
                for m in range(NX, 2 * NX):
                    step(m, it)
            for m in range(NX * (full + 1), SLOTS + lags):
                step(m, 0)

        def later(j, k, it):
            return j >= k or looped(it)

        def live(m, lag):
            return 0 <= m - lag < SLOTS

        registers = [0]

        def register_of(eng, at, top):
            registers[0] += 1
            reg = eng.alloc_register(f"loaded{registers[0]}")
            eng.reg_load(reg, at)
            return eng.snap(reg, donate=True, min_val=0, max_val=top)

        def expert(eng, j, it):
            return register_of(eng, ET[0:1, ds(j + NX * it, 1)] if looped(it) else ET[0:1, j:j + 1], E - 1)

        def fill_tails(eng, r, experts_):
            eng.wait_ge(tail_ready[r], 1)
            for e in experts_:
                row = register_of(eng, TAIL[0:1, e:e + 1], E * REGION * P - P)
                eng.dma_start(slots[r][ds(row, P), :], FILL[:, :]).then_inc(tail_filled[r], 16)

        def apart(eng, passed):
            eng.sem_inc(passed, 1)

        @block.sync
        def _(sp):
            def load_x(t0, t1, k):
                sp.dma_start(ROWS[:, t0:t1, 0:D], x_rows[:, t0:t1, :]).then_inc(x_in[k], 16)

            load_x(0, G, 0)
            load_x(G, 2 * G, 1)
            sp.dma_start(CTX[:, :, :], context.rearrange("b m c -> (b m) c").rearrange("(k p) c -> p k c", p=P))\
                .then_inc(attw_in, 16)
            sp.dma_start(WKR[:, :, :], Wk.rearrange("c (h q) -> c h q", h=H)).then_inc(attw_in, 16)
            sp.dma_start(WVR[:, :, :], Wv.rearrange("c (h q) -> c h q", h=H)).then_inc(attw_in, 16)
            sp.dma_start(WQR[:, :, :], Wq.rearrange("d (h q) -> d h q", h=H)).then_inc(attw_in, 16)
            sp.dma_start(WOR[:, :, :], Wout.rearrange("(h p) q -> p h q", h=H)).then_inc(attw_in, 16)
            sp.dma_start(WRAW[:, 0, :], w1[0]).then_inc(w1_in[0], 16)
            load_x(2 * G, T, 2)
            sp.dma_start(WRAW[:, 1:E, :], w1[1:E].rearrange("e d f -> d e f")).then_inc(w1_in[1], 16)
            sp.wait_ge(fill_ready, 1)
            for r in range(2):
                sp.dma_start(slots[r][E * REGION * P:, :].rearrange("(j p) w -> p j w", p=P),
                             FILL[:, :].unsqueeze(1).to_broadcast([P, EMPTY, ROW])).then_inc(slots_filled, 16)
            for e in range(E):
                if e == E - 1:
                    sp.wait_ge(prep_qk_ps, H)
                    sp.wait_ge(prep_v_ps, H)
                    sp.dma_start(B1[:, 0:B1_EARLY, :], b1[0:B1_EARLY].partition_broadcast(P)).then_inc(b1_in[0], 16)
                sp.wait_ge(w1_lo, e + 1)
                sp.dma_start(WRAW[:, e, :].rearrange("p (c d) -> p c d", c=FC),
                             w2[e].rearrange("(c p) d -> p c d", p=P)).then_inc(w2_in[e], 16)

            def experts(r):
                if r == 0:
                    sp.wait_ge(vw_ps, H)
                else:
                    sp.wait_ge(pT_hi, UNITS + LAG_AV - LAG_T)
                    sp.wait_ge(pT_lo, UNITS + LAG_AV - LAG_T - 1)
                    sp.wait_ge(av, UNITS)
                if r == 0:
                    fill_tails(sp, r, range(0, E, 2))
                sp.dma_start(B2[:, :, :], b2.partition_broadcast(P)).then_inc(b2_in[r], 16)
                first = B1_EARLY if r == 0 else 0
                sp.dma_start(B1[:, first:E, :], b1[first:E].partition_broadcast(P)).then_inc(b1_in[r], 16)
                if r == 1:
                    fill_tails(sp, r, range(0, E, 2))
                if r == 0:
                    sp.wait_ge(w2_lo, E)
                sp.wait_ge(slots_filled, 32)
                sp.wait_ge(routed[r], 1)
                sp.wait_ge(tail_filled[r], 16 * E)
                for k in range(2):
                    sp.wait_ge(sorted_rows[k], 16 * T // 2 * (r + 1))

                slot_tiles = slots[r].rearrange("(j p) w -> p j w", p=P)

                def load(m, it):
                    if not live(m, 0):
                        return
                    at = TB[0:1, ds(m + NX * it, 1)] if looped(it) else TB[0:1, m:m + 1]
                    block_ = register_of(sp, at, E * REGION + EMPTY - 1)
                    if later(m, NX, it):
                        sp.wait_ge(s_x2[r], m - NX + 1 + NX * it)
                        sp.wait_ge(s_ids[r], m - NX + 1 + NX * it)
                    sp.dma_start(XS[:, m % NX:m % NX + 1, :], slot_tiles[:, ds(block_, 1), :])\
                        .then_inc(slot_in[r][m % NX], 16)

                tiles(sp, load, 0)

            experts(0)
            for k in range(NX):
                sp.wait_ge(slot_out[0][k], 16 * ((SLOTS - 1 - k) // NX + 1))
            sp.dma_start(ROWS[:, 0:G, 0:D], x1_rows[:, 0:G, :]).then_inc(x1_in[0], 16)
            sp.dma_start(ROWS[:, G:T, 0:D], x1_rows[:, G:T, :]).then_inc(x1_in[1], 16)
            experts(1)
            for k in range(NX):
                sp.wait_ge(slot_out[1][k], 16 * ((SLOTS - 1 - k) // NX + 1))

        @block.gpsimd
        def _(pool):
            pool.memset(IDN[:, :], 0.0).then_inc(memsets, 1)
            pool.memset(BEFORE[:, :], 0.0).then_inc(memsets, 1)
            pool.memset(FILL[:, :], 0.0).then_inc(memsets, 1)
            pool.memset(ONES[:, :], 1.0)
            pool.memset(NHALF[:, :], -0.5).then_inc(memsets, 1)
            pool.memset(ONF[:, :], 1.0)
            for r in range(2):
                pool.memset(OH[r][0][:, :, 0:1], 0.0)
            pool.wait_ge(memsets, 4)
            pool.affine_select(out=IDN[:, :], in_=IDN[:, :], compare_op=ALU.not_equal, fill=1.0, base=0,
                               pattern=[[-1, P]], channel_multiplier=1)
            pool.affine_select(out=BEFORE[:, :], in_=BEFORE[:, :], compare_op=ALU.is_ge, fill=1.0, base=0,
                               pattern=[[-1, P]], channel_multiplier=1)
            pool.iota(PREF[:, :], pattern=[[-1, E]], base=E, channel_multiplier=0,
                      allow_small_or_imprecise_dtypes=True)
            pool.iota(BASE[:, :, :], pattern=[[REGION, E], [0, G]], base=0, channel_multiplier=0,
                      allow_small_or_imprecise_dtypes=True)
            pool.iota(BASER[:, :], pattern=[[REGION * P, E]], base=0, channel_multiplier=0,
                      allow_small_or_imprecise_dtypes=True)
            pool.iota(TIDX[:, :], pattern=[[1, SLOTS]], base=0, channel_multiplier=0,
                      allow_small_or_imprecise_dtypes=True).then_inc(consts_ready, 1)
            pool.iota(FILL[:, ID:ID + 1].bitcast(i32), pattern=[[0, 1]], base=N, channel_multiplier=0)\
                .then_inc(fill_ready, 1)
            pool.iota(ROWS[:, :, ID].bitcast(i32), pattern=[[1, T]], base=0, channel_multiplier=T)\
                .then_inc(consts_ready, 1)

            def rstd(kind, job):
                pool.wait_ge(ln_ve[kind], job + 1)
                pool.tensor_tensor(RS[kind][:, :], VE[kind][:, :], NHALF[:, :], ALU.pow).then_inc(ln_rstd[kind], 1)

            def sort_tile(r, job, k, i, rows):
                if i == 0:
                    pool.wait_ge(pos_ready, job + 1)
                    pool.wait_ge(ln_keep, job + 1)
                    apart(pool, pool_passed)
                pool.indirect_dma_start(slots[r][:, :], bass.IndirectOffsetOnAxis(ap=POS[k][:, i:i + 1], axis=0),
                                        rows, None).then_inc(sorted_rows[k], 16)

            rstd(GATE, 0)
            rstd(GATE, 1)
            for g in range(NG):
                if g + 2 < NG:
                    rstd(GATE, g + 2)
                for i in range(G):
                    sort_tile(0, g, g % 2, i, ROWS[:, G * g + i, :])

            def experts(r):
                def step(m, it):
                    if live(m, 5):
                        j = m - 5
                        pool.wait_ge(s_xb[r], j + 1 + NX * it)
                        pool.wait_ge(s_ids[r], j + 1 + NX * it)
                        if later(j, NX, it):
                            pool.wait_ge(slot_out[r][j % NX], 16 * (j // NX) + 16 * it)
                        pool.tensor_tensor(RES[:, j % NX, :], XB2[:, j % 2, :], YT[:, j % 2, :], ALU.add)\
                            .then_inc(s_fin[r], 1)
                        pool.wait_ge(s_fin[r], j + 1 + NX * it)
                        apart(pool, pool_passed)
                        pool.indirect_dma_start(
                            ffn_dst[r], bass.IndirectOffsetOnAxis(ap=IDS[:, j % NX:j % NX + 1], axis=0),
                            RES[:, j % NX, :], None, bounds_check=N - 1, oob_is_err=False)\
                            .then_inc(slot_out[r][j % NX], 16)

                tiles(pool, step, 5)

            experts(0)
            rstd(ATT, 0)

            def slot(n, it):
                if n:
                    u = n - 1
                    pool.wait_ge(row_inv, u + 1 + BODY * it)
                    apart(pool, pool_passed)
                    pool.tensor_scalar(PR[:, u % 4, :], PR[:, u % 4, :], RI[:, u % 4:u % 4 + 1], 1.0,
                                       ALU.mult, ALU.mult).then_inc(normed, 1)
                for g in at_step(n, it, 12):
                    rstd(ATT, shifted(g + 1, it))
                for i in range(G):
                    for g in at_step(n, it, 14 + 2 * i, 2):
                        sort_tile(1, shifted(NG + g - 2, it), g % 2, i, X2[g % 2][:, i, :])
                for g in at_step(n, it, 28, 1):
                    rstd(GATE, shifted(NG + g - 1, it))

            rounds(pool, slot)
            rstd(GATE, 2 * NG - 1)
            for i in range(G):
                sort_tile(1, 2 * NG - 2, 0, i, X2[0][:, i, :])
            for i in range(G):
                sort_tile(1, 2 * NG - 1, 1, i, X2[1][:, i, :])
            experts(1)

        @block.scalar
        def _(act):
            act.dma_start(GWR[:, :], gate_w).then_inc(small_in, 16)
            act.dma_start(GB[:, :], gate_b.partition_broadcast(P)).then_inc(small_in, 16)
            act.dma_start(EB[:, :], expert_bias.partition_broadcast(P)).then_inc(small_in, 16)
            act.dma_start(BO[:, :], bout.rearrange("(d a) -> d a", a=1)).then_inc(small_in, 16)

            def norm(kind, job, rows, tiles_):
                act.wait_ge(ln_shift[kind], job + 1)
                if kind == ATT:
                    act.wait_ge(ln_T[GATE], job + NG - 2 if looped(job) or job >= 2 else NG)
                elif looped(job) or job >= NG:
                    act.wait_ge(ln_T[ATT], job - NG + 3 if looped(job) or job < 2 * NG - 1 else NG + 1)
                elif job:
                    act.wait_ge(ln_T[GATE], job)
                for i in tiles_:
                    last = act.activation(XN[:, i, :], rows(i), ACT.Identity, bias=SH[kind][:, i:i + 1],
                                          scale=RS[kind][:, i:i + 1])
                if i == G - 1:
                    last.then_inc(ln_xn[kind], 1)

            def rows_at(t0):
                return lambda i: (ROWS[:, t0 + i, 0:D] if isinstance(t0, int) else
                                  ROWS[:, ds(t0 + i, 1), 0:D].rearrange("p a d -> p (a d)"))

            def x2_at(k):
                return lambda i: X2[k][:, i, 0:D]

            def raw_evac(job, bank):
                act.wait_ge(ln_T[GATE], job + 1)
                if isinstance(job, int) and job < NG:
                    if job:
                        act.wait_ge(logit_ps, job)
                else:
                    act.wait_ge(oT_ps, job - NG + 1)
                act.activation(XNT[:, :], BK[bank][:, :], ACT.Copy).then_inc(raw_T, 1)

            def qk(h):
                act.wait_ge(prep_qk_ps, h + 1)
                if h:
                    act.wait_ge(m_ps, h)
                act.activation(WQT[:, :], BK[0][:, 0:P], ACT.Copy)
                act.activation(KT[:, :], BK[1][:, :], ACT.Copy).then_inc(prep_qk, 1)
                act.wait_ge(prep_v_ps, h + 1)
                if h:
                    act.wait_ge(vw_ps, h)
                act.activation(VT[:, :], BK[2][:, :], ACT.Copy).then_inc(prep_v, 1)

            def products(h):
                act.wait_ge(m_ps, h + 1)
                if h:
                    act.wait_ge(m_lo, h)
                act.activation(MT[:, :], BK[3][:, :], ACT.Copy, scale=SHARPEN * SCALE, accum_out=SM[:, 0:1])\
                    .then_inc(m_tmp, 1)
                act.wait_ge(vw_ps, h + 1)
                act.activation(VWH[:, h, :, :].rearrange("p c d -> p (c d)"), BK[4][:, :], ACT.Copy)\
                    .then_inc(vw_hi, 1)

            def w2_high(e):
                act.wait_ge(w2_in[e], 16)
                act.activation(W2HL[:, e, :, 0, :], WRAW[:, e, :].rearrange("p (c d) -> p c d", c=FC), ACT.Copy)\
                    .then_inc(w2_hi, 1)

            act.wait_ge(x_in[0], 16)
            norm(GATE, 0, rows_at(0), range(G))
            raw_evac(0, 6)
            act.wait_ge(ctxT_ps, 1)
            act.activation(CTXT[:, :], BK[5][0:C, :], ACT.Copy).then_inc(ctxT_ready, 1)
            qk(0)
            for s in range(NG):
                if s + 1 < NG:
                    act.wait_ge(x_in[min(s + 1, 2)], 16)
                    norm(GATE, s + 1, rows_at(G * (s + 1)), range(G))
                products(s)
                if s + 1 < NG:
                    raw_evac(s + 1, 6)
                    qk(s + 1)
                act.wait_ge(w1_in[min(s, 1)], 16)
                act.activation(W1H[:, s, :], WRAW[:, s, :], ACT.Copy).then_inc(w1_hi, 1)
                if s >= 2:
                    w2_high(s - 2)
            w2_high(E - 2)
            fill_tails(act, 0, range(1, E, 2))
            w2_high(E - 1)

            def experts(r):
                def slot_norm(m, it):
                    act.wait_ge(slot_in[r][m % NX], 16 * (m // NX + 1) + 16 * it)
                    if later(m, 2, it):
                        act.wait_ge(s_xT[r], m - 1 + NX * it)
                    act.activation(XSN[:, m % 2, :], XS[:, m % NX, 0:D], ACT.Identity,
                                   bias=XS[:, m % NX, SHIFT:SHIFT + 1], scale=XS[:, m % NX, RSTD:RSTD + 1])\
                        .then_inc(s_xn[r], 1)

                def step(m, it):
                    if live(m, 5):
                        j = m - 5
                        act.wait_ge(s_y[r], j + 1 + NX * it)
                        if later(j, 2, it):
                            act.wait_ge(s_fin[r], j - 1 + NX * it)
                        act.activation(YT[:, j % 2, :], BK[6 + j % 2][:, D:2 * D], ACT.Copy, scale=0.5)\
                            .then_inc(s_yb[r], 1)
                    if live(m, 3):
                        j = m - 3
                        act.wait_ge(s_hT[r], j + 1 + NX * it)
                        if later(j, 2, it):
                            act.wait_ge(s_y[r], j - 1 + NX * it)
                        act.activation(HTH[:, j % 2, :], BK[4 + j % 2][:, :], ACT.Relu).then_inc(s_hhi[r], 1)
                    if live(m, 0):
                        act.wait_ge(s_xT[r], m + 1 + NX * it)
                        if later(m, 2, it):
                            act.wait_ge(s_h[r], m - 1 + NX * it)
                        act.activation(XTH[:, m % 2, :], BK[m % 2][:, 0:P], ACT.Copy).then_inc(s_xhi[r], 1)
                    if live(m, -1):
                        slot_norm(m + 1, it)

                if r == 1:
                    fill_tails(act, r, range(1, E, 2))
                slot_norm(0, 0)
                tiles(act, step, 5)

            experts(0)

            act.wait_ge(x1_in[0], 16)
            norm(ATT, 0, rows_at(0), range(G))

            def xT_evac(g, it):
                act.wait_ge(ln_T[ATT], shifted(g, it) + 1)
                act.activation(AXH[:, g % 2, :], BK[6][:, :], ACT.Copy).then_inc(xT_hi, 1)

            xT_evac(0, 0)

            def slot(n, it):
                act.wait_ge(neg_max, n + 1 + BODY * it)
                if n >= 4:
                    act.wait_ge(pT_ps, n - 3 + BODY * it)
                act.activation(PR[:, n % 4, :], BK[n % 2][:, :], ACT.Exp, bias=NM[:, n % 4:n % 4 + 1],
                               accum_out=SU[:, n % 4:n % 4 + 1]).then_inc(probs, 1)
                if n >= LAG_T:
                    u = n - LAG_T
                    act.wait_ge(pT_ps, u + 1 + BODY * it)
                    if u % G == 0 and (u // G >= 2 or looped(it)):
                        act.wait_ge(av, G * (u // G) - G + BODY * it)
                    act.activation(PTH[:, (u // G) % 2, :, (u % G) * P:(u % G + 1) * P],
                                   BK[2 + u % 2][:, :].rearrange("p (c q) -> p c q", c=KC), ACT.Copy)\
                        .then_inc(pT_hi, 1)
                for i in range(G):
                    for g in at_step(n, it, 14 + i):
                        norm(ATT, shifted(g + 1, it), rows_at(group_tile(g + 1, it)), [i])
                for g in at_step(n, it, 20):
                    xT_evac(g + 1, it)
                for g in at_step(n, it, 8, 1):
                    o_evac(g - 1, it)
                for i in range(2):
                    for g in at_step(n, it, 30 + i, 1):
                        norm(GATE, shifted(NG + g - 1, it), x2_at((g - 1) % 2), [i])
                    for g in at_step(n, it, i, 2):
                        norm(GATE, shifted(NG + g - 2, it), x2_at(g % 2), [2 + i])
                for g in at_step(n, it, 3, 2):
                    raw_evac(shifted(NG + g - 2, it), 7)

            def o_evac(g, it):
                act.wait_ge(av, HG * (g + 1) + BODY * it)
                act.wait_ge(logit_ps, NG + g + 2 * it)
                act.activation(XNT[:, :], BK[4 + g % 2][:, :], ACT.Identity, bias=BO[:, 0:1]).then_inc(o_kept, 1)

            rounds(act, slot)
            o_evac(NG - 1, 0)
            norm(GATE, 2 * NG - 1, x2_at(1), range(G))
            raw_evac(2 * NG - 1, 7)
            experts(1)

        @block.vector
        def _(dve):
            v = nc.vector

            def row_of(t):
                return ROWS[:, t, 0:D] if isinstance(t, int) else ROWS[:, ds(t, 1), 0:D].rearrange("p a d -> p (a d)")

            def rows_at(t0):
                return lambda i: row_of(t0 + i)

            def x2_at(k):
                return lambda i: X2[k][:, i, 0:D]

            def stats(kind, job, rows, tiles_):
                apart(dve, dve_passed)
                for i in tiles_:
                    last = v.bn_stats(BN[kind][:, i, :], rows(i))
                if i == G - 1:
                    last.then_inc(ln_bn[kind], 1)

            def moments(kind, job):
                dve.wait_ge(ln_bn[kind], job + 1)
                if looped(job) or job:
                    dve.wait_ge(ln_xn[kind], job)
                apart(dve, dve_passed)
                for i in range(G):
                    last = v.bn_aggr(MV[kind][:, i, :], BN[kind][:, i, :])
                last.then_inc(ln_agg[kind], 1)
                dve.wait_ge(ln_agg[kind], job + 1)
                v.tensor_scalar(VE[kind][:, :], MV[kind][:, :, 1], EPS, None, ALU.add).then_inc(ln_ve[kind], 1)

            def shift(kind, job, span=None, t0=None):
                dve.wait_ge(ln_rstd[kind], job + 1)
                v.scalar_tensor_tensor(out=SH[kind][:, :], in0=MV[kind][:, :, 0], scalar=-1.0, in1=RS[kind][:, :],
                                       op0=ALU.mult, op1=ALU.mult).then_inc(ln_shift[kind], 1)
                if kind == GATE:
                    dve.wait_ge(ln_shift[kind], job + 1)
                    v.tensor_copy(span[:, :, SHIFT:SHIFT + 1], SH[kind][:, :].unsqueeze(2))
                    if t0 is not None:
                        ids = ROWS[:, t0:t0 + G, ID:ID + 1] if isinstance(t0, int) else ROWS[:, ds(t0, G), ID:ID + 1]
                        v.tensor_copy(span[:, :, ID:ID + 1].bitcast(i32), ids.bitcast(i32))
                    v.tensor_copy(span[:, :, RSTD:RSTD + 1], RS[kind][:, :].unsqueeze(2)).then_inc(ln_keep, 1)

            CHAIN = 6

            def onehot(r, job, k, steps):
                bias = lambda b: b[:, :].unsqueeze(1).to_broadcast([P, G, E])
                over = lambda: MX[:, :].unsqueeze(2).to_broadcast([P, G, E])
                lg = LG[:, :, :]
                mine = OH[r][k]
                for i in steps:
                    if i == 0:
                        dve.wait_ge(logit_ps, job + 1)
                    elif i < 7:
                        dve.wait_ge(onehot_step, CHAIN * job + i)
                    if i == 0:
                        v.tensor_tensor(lg, BK[7][:, 0:G * E].rearrange("p (t e) -> p t e", e=E), bias(GB), ALU.add)\
                            .then_inc(onehot_step, 1)
                    elif i == 1:
                        v.tensor_tensor(lg, lg, bias(EB), ALU.add).then_inc(onehot_step, 1)
                    elif i == 2:
                        v.tensor_reduce(MX[:, :], lg, AX.X, ALU.max).then_inc(onehot_step, 1)
                    elif i == 3:
                        v.tensor_tensor(lg, lg, over(), ALU.is_ge).then_inc(onehot_step, 1)
                    elif i == 4:
                        v.tensor_tensor(lg, lg, bias(PREF), ALU.mult).then_inc(onehot_step, 1)
                    elif i == 5:
                        v.tensor_reduce(MX[:, :], lg, AX.X, ALU.max).then_inc(onehot_step, 1)
                    elif i == 6:
                        v.tensor_tensor(mine[:, :, 1:1 + G].rearrange("p e t -> p t e"), lg, over(), ALU.is_equal)\
                            .then_inc(onehot_ready, 1)
                    elif i == 7:
                        dve.wait_ge(onehot_ready, job + 1)
                        with nc.allow_low_precision(reason="whole numbers up to T are exact"):
                            v.tensor_reduce(OH[r][1 - k][:, :, 0], mine[:, :, :], AX.X, ALU.add)\
                                .then_inc(sum_ready, 1)

            def positions(r, job, k, earlier, steps):
                for i in steps:
                    if i == 0:
                        dve.wait_ge(rank_ps, job + 1)
                        v.tensor_tensor(WRK[:, :, :], BK[RANK_BANK[r]][:, RANKS:RANKS + E * G].rearrange("p (e t) -> p e t", e=E),
                                        OH[r][k][:, :, 1:1 + G], ALU.mult).then_inc(ranked, 1)
                    elif i == 1:
                        dve.wait_ge(ranked, job + 1)
                        v.tensor_reduce(POSF[:, :], WRK[:, :, :].rearrange("p e t -> p t e"), AX.X, ALU.add)\
                            .then_inc(pos_step, 1)
                    else:
                        dve.wait_ge(pos_step, job + 1)
                        if looped(earlier) or earlier:
                            dve.wait_ge(sorted_rows[k], 16 * G * earlier)
                        v.tensor_copy(POS[k][:, :], POSF[:, :]).then_inc(pos_ready, 1)

            def table(r):
                step = [0]

                def link(ins):
                    step[0] += 1
                    ins.then_inc(table_step[r], 1)
                    dve.wait_ge(table_step[r], step[0])

                dve.wait_ge(total_ps[r], 1)
                total = BK[RANK_BANK[r]][:, TOTALS:TOTALS + E]
                tiles_of, ends, skip = (CNT[:, i, :] for i in range(3))
                per_tile = lambda a: a.unsqueeze(1).to_broadcast([P, SLOTS, E])
                v.tensor_tensor(TAIL[:, :], total, BASER[:, :], ALU.add).then_inc(tail_ready[r], 1)
                link(v.tensor_scalar(CNTI[:, 0, :], total, float(P - 1), None, ALU.add))
                link(v.tensor_scalar(CNTI[:, 1, :], CNTI[:, 0, :], 7, None, ALU.arith_shift_right))
                link(v.tensor_copy(tiles_of, CNTI[:, 1, :]))
                link(v.tensor_tensor_scan(ends, ONF[:, 0:1].to_broadcast([P, E]), tiles_of, 0.0, ALU.mult, ALU.add))
                link(v.tensor_scalar(skip, tiles_of, -1.0, float(REGION), ALU.mult, ALU.add))
                link(v.tensor_tensor(SEL[:, :, :], per_tile(ends), TIDX[:, :].unsqueeze(2).to_broadcast([P, SLOTS, E]),
                                     ALU.is_le))
                link(v.tensor_reduce(ETF[:, :], SEL[:, :, :], AX.X, ALU.add))
                link(v.tensor_scalar(ET[:, :], ETF[:, :], float(E - 1), None, ALU.min))
                link(v.tensor_tensor(SEL[:, :, :], SEL[:, :, :], per_tile(skip), ALU.mult))
                link(v.tensor_reduce(ETF[:, :], SEL[:, :, :], AX.X, ALU.add))
                v.tensor_tensor(TB[:, :], ETF[:, :], TIDX[:, :], ALU.add).then_inc(routed[r], 1)

            def experts(r):
                dve.wait_ge(b2_in[r], 16)
                v.tensor_scalar(B2[:, :, :], B2[:, :, :], 0.5, None, ALU.mult).then_inc(bias_half[r], 1)
                dve.wait_ge(bias_half[r], 1)

                def step(m, it):
                    if m == 2:
                        dve.wait_ge(b1_in[r], 16 * (2 - r))
                    if live(m, 2):
                        j = m - 2
                        e = expert(dve, j, it)
                        dve.wait_ge(s_h[r], j + 1 + NX * it)
                        if later(j, 3, it):
                            dve.wait_ge(s_hT[r], j - 2 + NX * it)
                        v.tensor_tensor(HB[:, j % 3, :].unsqueeze(1), BK[2 + j % 2][:, :].unsqueeze(1),
                                        B1[:, ds(e, 1), :], ALU.add).then_inc(s_hb[r], 1)
                        if later(j, NX, it):
                            dve.wait_ge(s_xb[r], j - NX + 1 + NX * it)
                        v.tensor_tensor(XB[:, j % NX, :].unsqueeze(1), XS[:, j % NX, 0:D].unsqueeze(1),
                                        B2[:, ds(e, 1), :], ALU.add).then_inc(s_x2[r], 1)
                    if live(m, 3):
                        j = m - 3
                        dve.wait_ge(s_hhi[r], j + 1 + NX * it)
                        v.scalar_tensor_tensor(out=HTL[:, j % 2, :], in0=BK[4 + j % 2][:, :], scalar=0.0,
                                               in1=HTH[:, j % 2, :].bitcast(fp32), op0=ALU.max,
                                               op1=ALU.subtract).then_inc(s_hlo[r], 1)
                    if live(m, 0):
                        dve.wait_ge(s_xhi[r], m + 1 + NX * it)
                        v.tensor_tensor(XTL[:, m % 2, :], BK[m % 2][:, 0:P], XTH[:, m % 2, :].bitcast(fp32),
                                        ALU.subtract).then_inc(s_xlo[r], 1)
                    if live(m, 4):
                        j = m - 4
                        dve.wait_ge(slot_in[r][j % NX], 16 * (j // NX + 1) + 16 * it)
                        if later(j, NX, it):
                            dve.wait_ge(slot_out[r][j % NX], 16 * (j // NX) + 16 * it)
                        v.tensor_copy(IDS[:, j % NX:j % NX + 1], XS[:, j % NX, ID:ID + 1].bitcast(i32))\
                            .then_inc(s_ids[r], 1)
                    if live(m, 5):
                        j = m - 5
                        dve.wait_ge(s_yb[r], j + 1 + NX * it)
                        dve.wait_ge(s_x2[r], j + 1 + NX * it)
                        v.scalar_tensor_tensor(out=XB2[:, j % 2, :], in0=BK[6 + j % 2][:, 0:D], scalar=0.5,
                                               in1=XB[:, j % NX, :], op0=ALU.mult, op1=ALU.add).then_inc(s_xb[r], 1)

                tiles(dve, step, 5)

            def w1_low(e):
                dve.wait_ge(w1_hi, e + 1)
                v.tensor_tensor(W1L[:, e, :], WRAW[:, e, :], W1H[:, e, :].bitcast(fp32), ALU.subtract)\
                    .then_inc(w1_lo, 1)

            def w2_low(e):
                dve.wait_ge(w2_hi, e + 1)
                v.tensor_tensor(W2HL[:, e, :, 1, :], WRAW[:, e, :].rearrange("p (c d) -> p c d", c=FC),
                                W2HL[:, e, :, 0, :].bitcast(fp32), ALU.subtract).then_inc(w2_lo, 1)

            def head(h):
                dve.wait_ge(m_tmp, h + 1)
                v.tensor_scalar(SM[:, 1:2], SM[:, 0:1], -(SHARPEN - 1.0) / (SHARPEN * KEYS), None, ALU.mult)\
                    .then_inc(m_shift, 1)
                dve.wait_ge(m_shift, h + 1)
                v.tensor_scalar(MH[:, h, :], MT[:, :], SM[:, 1:2], None, ALU.add).then_inc(m_hi, 1)
                dve.wait_ge(m_hi, h + 1)
                v.scalar_tensor_tensor(out=ML[:, h, :], in0=MT[:, :], scalar=SM[:, 1:2],
                                       in1=MH[:, h, :].bitcast(fp32), op0=ALU.add, op1=ALU.subtract).then_inc(m_lo, 1)
                dve.wait_ge(vw_hi, h + 1)
                v.tensor_tensor(VWL[:, h, :, :].rearrange("p c d -> p (c d)"), BK[4][:, :],
                                VWH[:, h, :, :].rearrange("p c d -> p (c d)").bitcast(fp32), ALU.subtract)\
                    .then_inc(vw_lo, 1)

            def ln_start(g):
                dve.wait_ge(x_in[min(g, 2)], 16)
                stats(GATE, g, rows_at(G * g), range(G))
                moments(GATE, g)

            def ln_end(g):
                shift(GATE, g, ROWS[:, G * g:G * g + G, :])

            ln_start(0)
            dve.wait_ge(consts_ready, 2)
            ln_end(0)
            ln_start(1)
            dve.wait_ge(gate_ps, 1)
            v.tensor_copy(GWT[:, :], BK[5][:, 0:E]).then_inc(gate_ready, 1)
            ln_end(1)
            dve.wait_ge(small_in, 64)
            for s in range(NG):
                onehot(0, s, s % 2, range(8))
                if s + 2 < NG:
                    ln_start(s + 2)
                if s == 0:
                    positions(0, s, s % 2, s // 2, range(3))
                    ln_end(s + 2)
                head(s)
                if s:
                    positions(0, s, s % 2, s // 2, range(3))
                    if s + 2 < NG:
                        ln_end(s + 2)
                w1_low(s)
                if s == NG - 1:
                    table(0)
                if s >= 2:
                    w2_low(s - 2)
            for e in range(E - 2, E):
                w2_low(e)

            experts(0)

            def xT_low(g, it, cols):
                dve.wait_ge(xT_hi, g + 1 + 2 * it)
                last = v.tensor_tensor(AXL[:, g % 2, cols], BK[6][:, cols], AXH[:, g % 2, cols].bitcast(fp32),
                                       ALU.subtract)
                if cols.stop == G * P:
                    last.then_inc(xT_lo, 1)

            dve.wait_ge(x1_in[0], 16)
            stats(ATT, 0, rows_at(0), range(G))
            moments(ATT, 0)
            shift(ATT, 0)
            xT_low(0, 0, slice(0, G * P))

            def new_rows(g, it, i):
                dve.wait_ge(oT_ps, g + 1 + 2 * it)
                dve.wait_ge(sorted_rows[g % 2], 16 * G * ((NG + g) // 2 + it))
                v.tensor_tensor(X2[g % 2][:, i, 0:D], row_of(group_tile(g, it) + i), BK[7][:, i * D:(i + 1) * D],
                                ALU.add).then_inc(x2_ready, 1)

            def slot(n, it):
                dve.wait_ge(scores, n + 1 + BODY * it)
                v.tensor_reduce(NM[:, n % 4:n % 4 + 1], BK[n % 2][:, :], AX.X, ALU.max, negate=True)\
                    .then_inc(neg_max, 1)
                if n >= LAG_T + 1:
                    u = n - LAG_T - 1
                    dve.wait_ge(pT_hi, u + 1 + BODY * it)
                    at = (slice(None), (u // G) % 2, slice(None), slice((u % G) * P, (u % G + 1) * P))
                    v.tensor_tensor(PTL[at], BK[2 + u % 2][:, :].rearrange("p (c q) -> p c q", c=KC),
                                    PTH[at].bitcast(fp32), ALU.subtract).then_inc(pT_lo, 1)
                if n:
                    u = n - 1
                    dve.wait_ge(probs, u + 1 + BODY * it)
                    v.reciprocal(RI[:, u % 4:u % 4 + 1], SU[:, u % 4:u % 4 + 1]).then_inc(row_inv, 1)
                for i in range(G):
                    for g in at_step(n, it, 7 + i):
                        if n == 7 and not looped(it):
                            dve.wait_ge(x1_in[1], 16)
                        stats(ATT, shifted(g + 1, it), rows_at(group_tile(g + 1, it)), [i])
                for g in at_step(n, it, 11):
                    moments(ATT, shifted(g + 1, it))
                for g in at_step(n, it, 13):
                    shift(ATT, shifted(g + 1, it))
                for half in range(2):
                    for g in at_step(n, it, 21 + half):
                        xT_low(g + 1, it, slice(half * 2 * P, (half + 1) * 2 * P))
                for i in range(G):
                    for g in at_step(n, it, 15 + i, 1):
                        new_rows(g - 1, it, i)
                for i in range(G):
                    for g in at_step(n, it, 23 + i, 1):
                        dve.wait_ge(x2_ready, G * shifted(g - 1, it) + i + 1)
                        stats(GATE, shifted(NG + g - 1, it), x2_at((g - 1) % 2), [i])
                for g in at_step(n, it, 27, 1):
                    moments(GATE, shifted(NG + g - 1, it))
                for g in at_step(n, it, 29, 1):
                    shift(GATE, shifted(NG + g - 1, it), X2[(g - 1) % 2][:, :, :], group_tile(g - 1, it))
                for i in range(3):
                    for g in at_step(n, it, 5 + i, 2):
                        onehot(1, shifted(NG + g - 2, it), g % 2, range(3 * i, min(3 * i + 3, 8)))
                for i in range(3):
                    for g in at_step(n, it, 11 + i, 2):
                        positions(1, shifted(NG + g - 2, it), g % 2, shifted((NG + g - 2) // 2, it, 1), [i])

            rounds(dve, slot)
            positions(1, 2 * NG - 2, 0, NG - 1, range(3))
            for i in range(G):
                new_rows(NG - 1, 0, i)
            dve.wait_ge(x2_ready, T)
            stats(GATE, 2 * NG - 1, x2_at(1), range(G))
            moments(GATE, 2 * NG - 1)
            shift(GATE, 2 * NG - 1, X2[1][:, :, :], T - G)
            onehot(1, 2 * NG - 1, 1, range(8))
            positions(1, 2 * NG - 1, 1, NG - 1, range(3))
            table(1)
            experts(1)

        @block.tensor
        def _(pe):
            def xn_transposes(kind, job, bank):
                pe.wait_ge(ln_xn[kind], job + 1)
                for i in range(G):
                    last = pe.transpose(BK[bank][:, i * P:(i + 1) * P], XN[:, i, :], IDN[:, :])
                last.then_inc(ln_T[kind], 1)

            def gate_logits(job):
                pe.wait_ge(raw_T, job + 1)
                for i in range(G):
                    last = pe.matmul(BK[7][:, i * E:(i + 1) * E], XNT[:, i * P:(i + 1) * P], GWT[:, :],
                                     start=True, stop=True)
                last.then_inc(logit_ps, 1)

            def ranks(r, job, k):
                pe.wait_ge(onehot_ready, job + 1)
                if looped(job) or job:
                    pe.wait_ge(sum_ready, job)
                    pe.wait_ge(ranked, job)
                out = BK[RANK_BANK[r]][:, RANKS:RANKS + E * G].rearrange("p (e t) -> p e t", e=E)
                mine = OH[r][k]
                pe.matmul(out, ONES[:, :], BASE[:, :, :], start=True, stop=False)
                for i in range(G):
                    pe.matmul(out[:, :, i:G], ONES[:, :], mine[:, :, i:i + 1].to_broadcast([P, E, G - i]),
                              start=False, stop=False)
                pe.matmul(out, BEFORE[:, :], mine[:, :, 1:1 + G], start=False, stop=True).then_inc(rank_ps, 1)

            def totals(r):
                pe.wait_ge(sum_ready, NG * (r + 1))
                pe.wait_ge(ranked, NG * (r + 1))
                pe.matmul(BK[RANK_BANK[r]][:, TOTALS:TOTALS + E], ONES[:, :], OH[r][0][:, :, 0], start=True, stop=True)\
                    .then_inc(total_ps[r], 1)

            def three(out, wh, wl, mh, ml, start, stop):
                pe.matmul(out, wh, mh, start=start, stop=False)
                pe.matmul(out, wh, ml, start=False, stop=False)
                return pe.matmul(out, wl, mh, start=False, stop=stop)

            def experts(r):
                def step(m, it):
                    if m == 4 and r == 0:
                        pe.wait_ge(w2_lo, E)
                    if live(m, 4):
                        e2 = expert(pe, m - 4, it)
                    if live(m, 3):
                        j = m - 3
                        pe.wait_ge(s_hb[r], j + 1 + NX * it)
                        if later(j, 2, it):
                            pe.wait_ge(s_hlo[r], j - 1 + NX * it)
                        for c in range(FC):
                            last = pe.transpose(BK[4 + j % 2][:, c * P:(c + 1) * P], HB[:, j % 3, c * P:(c + 1) * P],
                                                IDN[:, :])
                        last.then_inc(s_hT[r], 1)
                    if live(m, 1):
                        e1 = expert(pe, m - 1, it)
                    if live(m, 4):
                        j = m - 4
                        pe.wait_ge(s_hlo[r], j + 1 + NX * it)
                        if later(j, 2, it):
                            pe.wait_ge(s_xb[r], j - 1 + NX * it)
                        for c in range(FC):
                            pe.matmul(BK[6 + j % 2][:, 0:2 * D].rearrange("p (a s d) -> p a s d", a=1, s=2),
                                      HTH[:, j % 2, c * P:(c + 1) * P], W2HL[:, ds(e2, 1), c, :, :],
                                      start=(c == 0), stop=False)
                            last = pe.matmul(BK[6 + j % 2][:, 0:D].unsqueeze(1), HTL[:, j % 2, c * P:(c + 1) * P],
                                             W2HL[:, ds(e2, 1), c, 0, :], start=False, stop=(c == FC - 1))
                        last.then_inc(s_y[r], 1)
                    if live(m, 0):
                        pe.wait_ge(s_xn[r], m + 1 + NX * it)
                        if later(m, 2, it):
                            pe.wait_ge(s_xlo[r], m - 1 + NX * it)
                        pe.transpose(BK[m % 2][:, 0:P], XSN[:, m % 2, :], IDN[:, :]).then_inc(s_xT[r], 1)
                    if live(m, 1):
                        j = m - 1
                        pe.wait_ge(s_xlo[r], j + 1 + NX * it)
                        if later(j, 2, it):
                            pe.wait_ge(s_hb[r], j - 1 + NX * it)
                        three(BK[2 + j % 2][:, :].unsqueeze(1), XTH[:, j % 2, :], XTL[:, j % 2, :],
                              W1H[:, ds(e1, 1), :], W1L[:, ds(e1, 1), :], True, True).then_inc(s_h[r], 1)

                tiles(pe, step, 4)

            pe.wait_ge(consts_ready, 2)
            pe.wait_ge(small_in, 64)
            pe.transpose(BK[5][:, 0:E], GWR[:, :], IDN[0:E, 0:E]).then_inc(gate_ps, 1)
            xn_transposes(GATE, 0, 6)
            pe.wait_ge(gate_ready, 1)
            gate_logits(0)
            pe.wait_ge(attw_in, 16 * 5)
            for c in range(KC):
                last = pe.transpose(BK[5][0:C, c * P:(c + 1) * P], CTX[:, c, :], IDN[:, :])
            last.then_inc(ctxT_ps, 1)
            pe.wait_ge(ctxT_ready, 1)

            def head_inputs(h):
                if h:
                    pe.wait_ge(prep_qk, h)
                    pe.wait_ge(prep_v, h)
                pe.transpose(BK[0][:, 0:P], WQR[:, h, :], IDN[:, :])
                pe.matmul(BK[1][:, :], WKR[:, h, :], CTXT[:, :], start=True, stop=True).then_inc(prep_qk_ps, 1)
                pe.matmul(BK[2][:, :], WVR[:, h, :], CTXT[:, :], start=True, stop=True).then_inc(prep_v_ps, 1)

            def head_products(h):
                pe.wait_ge(prep_qk, h + 1)
                if h:
                    pe.wait_ge(m_tmp, h)
                    pe.wait_ge(vw_lo, h)
                pe.matmul(BK[3][:, :], WQT[:, :], KT[:, :], start=True, stop=True).then_inc(m_ps, 1)
                pe.wait_ge(prep_v, h + 1)
                for c in range(KC):
                    last = pe.matmul(BK[4][:, c * D:(c + 1) * D], VT[:, c * P:(c + 1) * P], WOR[:, h, :],
                                     start=True, stop=True)
                last.then_inc(vw_ps, 1)

            head_inputs(0)
            for s in range(NG):
                head_products(s)
                if s + 1 < NG:
                    pe.wait_ge(raw_T, s + 1)
                    xn_transposes(GATE, s + 1, 6)
                ranks(0, s, s % 2)
                if s + 1 < NG:
                    head_inputs(s + 1)
                    pe.wait_ge(onehot_ready, s + 1)
                    gate_logits(s + 1)
            totals(0)

            pe.wait_ge(w1_lo, E)
            pe.wait_ge(vw_lo, H)
            pe.wait_ge(routed[0], 1)
            experts(0)

            pe.wait_ge(s_fin[0], SLOTS)
            xn_transposes(ATT, 0, 6)

            def slot(n, it):
                g = n // HG
                u = n
                h = (u // G) % H
                i = u % G
                if u % HG == 0:
                    pe.wait_ge(xT_lo, g + 1 + 2 * it)
                if u >= 2:
                    pe.wait_ge(probs, u - 1 + BODY * it)
                cols = slice(i * P, (i + 1) * P)
                three(BK[u % 2][:, :], AXH[:, g % 2, cols], AXL[:, g % 2, cols], MH[:, h, :], ML[:, h, :],
                      True, True).then_inc(scores, 1)
                if n >= LAG_AV:
                    u = n - LAG_AV
                    g, h, c = u // HG, (u // G) % H, u % G
                    hh = u // G
                    if c == 0:
                        pe.wait_ge(pT_lo, G * hh + G + BODY * it)
                        if h == 0 and (g >= 2 or looped(it)):
                            pe.wait_ge(o_kept, g - 1 + 2 * it)
                    three(BK[4 + g % 2][:, :], VWH[:, h, c, :], VWL[:, h, c, :], PTH[:, hh % 2, c, :],
                          PTL[:, hh % 2, c, :], h == 0 and c == 0, h == H - 1 and c == KC - 1).then_inc(av, 1)
                if n >= LAG_T:
                    u = n - LAG_T
                    pe.wait_ge(normed, u + 1 + BODY * it)
                    if u >= 2:
                        pe.wait_ge(pT_lo, u - 1 + BODY * it)
                    for c in range(KC):
                        last = pe.transpose(BK[2 + u % 2][:, c * P:(c + 1) * P], PR[:, u % 4, c * P:(c + 1) * P],
                                            IDN[:, :])
                    last.then_inc(pT_ps, 1)
                for g in at_step(n, it, 19):
                    pe.wait_ge(xT_lo, g + 1 + 2 * it)
                    xn_transposes(ATT, shifted(g + 1, it), 6)
                for g in at_step(n, it, 14, 1):
                    o_transposes(g - 1, it)
                for g in at_step(n, it, 2, 2):
                    xn_transposes(GATE, shifted(NG + g - 2, it), 7)
                for g in at_step(n, it, 4, 2):
                    gate_logits(shifted(NG + g - 2, it))
                for g in at_step(n, it, 10, 2):
                    ranks(1, shifted(NG + g - 2, it), g % 2)

            def o_transposes(g, it):
                pe.wait_ge(o_kept, g + 1 + 2 * it)
                pe.wait_ge(onehot_ready, NG + g + 2 * it)
                pe.wait_ge(ranked, NG + g + 2 * it)
                for i in range(G):
                    last = pe.transpose(BK[7][:, i * D:(i + 1) * D], XNT[:, i * P:(i + 1) * P], IDN[:, :])
                last.then_inc(oT_ps, 1)

            rounds(pe, slot)
            ranks(1, 2 * NG - 2, 0)
            o_transposes(NG - 1, 0)
            xn_transposes(GATE, 2 * NG - 1, 7)
            gate_logits(2 * NG - 1)
            ranks(1, 2 * NG - 1, 1)
            totals(1)
            pe.wait_ge(routed[1], 1)
            experts(1)


_INS = ["L0_attn_x", "L0_attn_context", "L0_attn_Wq", "L0_attn_Wk", "L0_attn_Wv", "L0_attn_Wout", "L0_attn_bout",
        "L0_ffn_gate_w", "L0_ffn_gate_b", "L0_ffn_expert_bias", "L0_ffn_w1", "L0_ffn_b1", "L0_ffn_w2", "L0_ffn_b2"]


def kernel(**inputs):
    import numpy as _np
    import concourse.bacc as _bacc
    from concourse import mybir as _mybir
    from concourse.bass_utils import run_bass_kernel_spmd as _run

    nc = _bacc.Bacc("TRN2", target_bir_lowering=False, num_devices=1)
    arrays, args = {}, []
    for name in _INS:
        a = _np.ascontiguousarray(inputs[name])
        arrays[f"in_{name}"] = a
        args.append(nc.dram_tensor(f"in_{name}", a.shape, _mybir.dt.from_np(a.dtype), kind="ExternalInput").ap())
    shape = tuple(inputs["L0_attn_x"].shape)
    out = nc.dram_tensor("out_0", shape, _mybir.dt.float32, kind="ExternalOutput").ap()
    macaron_kernel(nc, *args, out)
    r = _run(nc, [arrays], core_ids=[0])
    return r.results[0]["out_0"]
```

```python
import concourse.bass as bass
from concourse import mybir
from contextlib import ExitStack

P = 128
EPS = 1e-05


def macaron_kernel(nc, x, context, Wq, Wk, Wv, Wout, bout, gate_w, gate_b, expert_bias, w1, b1, w2, b2, out):
    fp32, f32r, i32, bf16 = (mybir.dt.float32, mybir.dt.float32r, mybir.dt.int32, mybir.dt.bfloat16)
    ALU = mybir.AluOpType
    ACT = mybir.ActivationFunctionType
    AX = mybir.AxisListType
    ds = bass.ds

    N = x.shape[0] * x.shape[1]
    D = x.shape[2]
    T = N // P
    KEYS = context.shape[0] * context.shape[1]
    KC = KEYS // P
    C = context.shape[2]
    H = Wq.shape[1] // D
    SCALE = float(D) ** -0.5
    SHARPEN = 1.5
    E, F = w1.shape[0], w1.shape[2]
    FC = F // P
    SLOTS = T + E - 1
    G = 4
    NG = T // G
    ROW = D + 3
    ID, SHIFT, RSTD = D, D + 1, D + 2

    x_rows = x.rearrange("b n d -> (b n) d").rearrange("(p t) d -> p t d", t=T)
    out_rows = out.rearrange("b n d -> (b n) d")
    x1 = nc.dram_tensor("x1", [N, D], fp32, kind="Internal").ap()
    REGION = T + 1
    EMPTY = SLOTS - T
    B1_EARLY = 3 * H * D // F
    slots = [nc.dram_tensor(f"slots{r}", [(E * REGION + EMPTY) * P, ROW], fp32, kind="Internal").ap()
             for r in range(2)]
    x1_rows = x1.rearrange("(p t) d -> p t d", t=T)
    ffn_dst = [x1, out_rows]

    ctx = ExitStack()
    with ctx:
        def sb(name, shape, dt, where=ctx):
            return where.enter_context(nc.sbuf_tensor(name, shape, dt))

        def sem(name):
            return ctx.enter_context(nc.semaphore(name))

        ROWS = sb("rows", [P, T, ROW], fp32)
        W1H = sb("w1_hi", [P, E, F], f32r)
        W1L = sb("w1_lo", [P, E, F], f32r)
        W2HL = sb("w2_hi_lo", [P, E, FC, 2, D], f32r)
        MH = sb("m_hi", [P, H, KEYS], f32r)
        ML = sb("m_lo", [P, H, KEYS], f32r)
        VWH = sb("vw_hi", [P, H, KC, D], f32r)
        VWL = sb("vw_lo", [P, H, KC, D], f32r)
        XN = sb("xn", [P, G, D], fp32)
        XNT = sb("xnT_or_oT", [P, G * P], fp32)
        X2 = [sb(f"x2_rows{k}", [P, G, ROW], fp32) for k in range(2)]
        IDN = sb("ident", [P, P], fp32)
        BEFORE = sb("before", [P, P], bf16)
        ONES = sb("ones", [P, P], bf16)
        FILL = sb("fill", [P, ROW], fp32)
        NHALF = sb("nhalf", [P, G], fp32)
        GWR = sb("gate_w", [E, D], fp32)
        GWT = sb("gate_wT", [P, E], fp32)
        GB = sb("gate_b", [P, E], fp32)
        EB = sb("expert_bias", [P, E], fp32)
        BO = sb("bout", [P, 1], fp32)
        PREF = sb("pref", [P, E], fp32)
        TIDX = sb("tile_index", [P, SLOTS], fp32)
        BN = [sb(f"bn{k}", [P, G, 6], fp32) for k in range(2)]
        MV = [sb(f"mean_var{k}", [P, G, 2], fp32) for k in range(2)]
        VE = [sb(f"var_eps{k}", [P, G], fp32) for k in range(2)]
        RS = [sb(f"rstd{k}", [P, G], fp32) for k in range(2)]
        SH = [sb(f"shift{k}", [P, G], fp32) for k in range(2)]
        LG = sb("logits", [P, G, E], fp32)
        MX = sb("row_max", [P, G], fp32)
        OH = [[sb(f"onehot{r}_{k}", [P, E, 1 + G], bf16) for k in range(2)] for r in range(2)]
        BASE = sb("region_base", [P, E, G], bf16)
        BASER = sb("region_row", [P, E], fp32)
        WRK = sb("route_work", [P, E, G], fp32)
        POSF = sb("pos_f", [P, G], fp32)
        POS = [sb(f"pos{k}", [P, G], i32) for k in range(2)]
        CNT = sb("counts", [P, 3, E], fp32)
        CNTI = sb("counts_int", [P, 2, E], i32)
        TAIL = sb("region_tail", [P, E], i32)
        ET = sb("expert_of_tile", [P, SLOTS], i32)
        TB = sb("block_of_tile", [P, SLOTS], i32)
        ETF = sb("tile_f", [P, SLOTS], fp32)
        SEL = sb("sel", [P, SLOTS, E], fp32)
        ONF = sb("ones_f", [P, 1], fp32)

        with ExitStack() as prep:
            WQR = sb("wq", [P, H, D], fp32, prep)
            WKR = sb("wk", [C, H, D], fp32, prep)
            WVR = sb("wv", [C, H, D], fp32, prep)
            WOR = sb("wout", [P, H, D], fp32, prep)
            CTX = sb("ctx", [P, KC, C], fp32, prep)
            CTXT = sb("ctxT", [C, KEYS], fp32, prep)
            WT = sb("wqT_wkT_wvT", [P, P + 2 * C], fp32, prep)
            WW = sb("wk_wqT_and_wv_wout", [C, 2, D], fp32, prep)
            CTXK = sb("ctxT_sharp", [C, KEYS], fp32, prep)
            CM = sb("ctx_mean", [C, 2], fp32, prep)
            WRAW = sb("w_raw", [P, E, F], fp32, prep)
        with ExitStack() as ffn:
            B1 = sb("b1", [P, E, F], fp32, ffn)
            B2 = sb("b2", [P, E, D], fp32, ffn)
            NX = 6
            RES = sb("result_rows", [P, NX, D], fp32, ffn)
            IDS = sb("result_ids", [P, NX], i32, ffn)
            XTH = sb("slot_xT_hi", [P, 2, P], f32r, ffn)
            XTL = sb("slot_xT_lo", [P, 2, P], f32r, ffn)
            HB = sb("h", [P, 3, F], fp32, ffn)
            HTH = sb("hT_hi", [P, 2, FC * P], f32r, ffn)
            HTL = sb("hT_lo", [P, 2, FC * P], f32r, ffn)
            XB = sb("x_b2", [P, NX, D], fp32, ffn)
            XB2 = sb("x_b2_y", [P, 2, D], fp32, ffn)
            YT = sb("y_lo_half", [P, 2, D], fp32, ffn)
            XS = sb("slot_rows", [P, NX, ROW], fp32, ffn)
            XSN = sb("slot_xn", [P, 2, D], fp32, ffn)
        with ExitStack() as att:
            PTH = sb("probsT_hi", [P, 2, KC, G * P], f32r, att)
            PTL = sb("probsT_lo", [P, 2, KC, G * P], f32r, att)
            PR = sb("probs", [P, 4, KEYS], fp32, att)
            AXH = sb("xT_hi", [P, 2, G * P], f32r, att)
            AXL = sb("xT_lo", [P, 2, G * P], f32r, att)
            NM = sb("neg_max", [P, 4], fp32, att)
            SU = sb("row_sum", [P, 4], fp32, att)
            RI = sb("row_inv", [P, 4], fp32, att)

        BK = [ctx.enter_context(nc.psum_tensor(f"bank{i}", [P, 512], fp32)) for i in range(8)]

        x_in = [sem(f"x_in{k}") for k in range(3)]
        small_in = sem("small_in")
        w1_in = [sem(f"w1_in{k}") for k in range(2)]
        w2_in = [sem(f"w2_in{e}") for e in range(E)]
        attw_in = sem("attw_in")
        slots_filled = sem("slots_filled")
        memsets = sem("memsets")
        consts_ready = sem("consts_ready")
        fill_ready = sem("fill_ready")
        gate_ps, gate_ready = sem("gate_ps"), sem("gate_ready")
        w1_hi, w1_lo, w2_hi, w2_lo = sem("w1_hi"), sem("w1_lo"), sem("w2_hi"), sem("w2_lo")
        ctxT_ps, ctxT_ready, ctx_mean, ctxK_ready = (sem("ctxT_ps"), sem("ctxT_ready"), sem("ctx_mean_ready"),
                                                    sem("ctxT_sharp_ready"))
        wT_ps, wT_ready, ww_ps, ww_ready = sem("wT_ps"), sem("wT_ready"), sem("ww_ps"), sem("ww_ready")
        m_ps, vw_ps = sem("m_ps"), sem("vw_ps")
        m_hi, m_lo = sem("m_hi"), sem("m_lo")
        vw_hi, vw_lo = sem("vw_hi"), sem("vw_lo")
        pool_passed, dve_passed = sem("pool_passed"), sem("dve_passed")
        ln_bn, ln_agg, ln_ve, ln_rstd, ln_shift, ln_xn, ln_T = (
            [sem(f"{n}{k}") for k in range(2)] for n in
            ("ln_bn", "ln_agg", "ln_ve", "ln_rstd", "ln_shift", "ln_xn", "ln_T"))
        ln_keep = sem("ln_keep")
        xn_first = sem("xn_first_half")
        raw_T, logit_ps = sem("raw_T"), sem("logit_ps")
        onehot_step, onehot_ready, sum_ready = sem("onehot_step"), sem("onehot_ready"), sem("sum_ready")
        rank_ps, ranked, pos_step, pos_ready = sem("rank_ps"), sem("ranked"), sem("pos_step"), sem("pos_ready")
        sorted_rows = [sem(f"sorted_rows{k}") for k in range(2)]
        total_ps = [sem(f"total_ps{r}") for r in range(2)]
        table_step = [sem(f"table_step{r}") for r in range(2)]
        tail_ready = [sem(f"tail_ready{r}") for r in range(2)]
        tail_filled = [sem(f"tail_filled{r}") for r in range(2)]
        routed = [sem(f"routed{r}") for r in range(2)]
        b1_in = [sem(f"b1_in{r}") for r in range(2)]
        b2_in = [sem(f"b2_in{r}") for r in range(2)]
        bias_half = [sem(f"bias_half{r}") for r in range(2)]
        slot_in = [[sem(f"slot_in{r}_{k}") for k in range(NX)] for r in range(2)]
        slot_out = [[sem(f"slot_out{r}_{k}") for k in range(NX)] for r in range(2)]
        s_xn, s_xT, s_xhi, s_xlo, s_h, s_hb, s_hT, s_hhi, s_hlo, s_y, s_xb, s_yb, s_fin, s_ids, s_x2 = (
            [sem(f"{n}{r}") for r in range(2)] for n in
            ("slot_xn_ready", "slot_xT_ps", "slot_xT_hi_ready", "slot_xT_lo_ready", "h_ps", "h_ready", "hT_ps",
             "hT_hi_ready", "hT_lo_ready", "y_ps", "y_hi_added", "y_lo_half", "slot_done", "ids_kept", "x_b2_ready"))
        s_close = [sem(f"closing_slot_done{r}") for r in range(2)]
        x1_in = [sem("x1_first"), sem("x1_rest")]
        xT_hi, xT_lo = sem("xT_hi_ready"), sem("xT_lo_ready")
        scores, neg_max, probs, row_inv, normed = (sem("scores"), sem("neg_max_ready"), sem("probs_ready"),
                                                   sem("row_inv_ready"), sem("probs_normed"))
        pT_ps, pT_hi, pT_lo, av = sem("probsT_ps"), sem("probsT_hi_ready"), sem("probsT_lo_ready"), sem("av_done")
        o_kept, oT_ps, x2_ready = sem("o_kept"), sem("oT_ps"), sem("x2_ready")

        block = ctx.enter_context(nc.Block())

        HG = H * G
        BODY = 2 * HG
        UNITS = NG * HG
        LAG_W2 = 2
        LAG_T, LAG_AV = 3, 8

        def looped(it):
            return not isinstance(it, int)

        def rounds(eng, slot):
            for n in range(BODY + LAG_AV):
                slot(n, 0)
            with eng.Fori(1, NG // 2) as it:
                for n in range(LAG_AV, BODY + LAG_AV):
                    slot(n, it)

        def at_step(n, it, s, back=0):
            return [n // HG] if n % HG == s and (n // HG >= back or looped(it)) else []

        def group_tile(g, it):
            return (G * g + 2 * G * it) % T if looped(it) else G * g

        GATE, ATT = 0, 1
        RANKS, TOTALS = 0, 64
        RANK_BANK = [5, 7]

        def shifted(g, it, k=2):
            return g + k * it if looped(it) else g

        def tiles(eng, step, lags):
            full = (SLOTS - NX) // NX
            for m in range(2 * NX):
                step(m, 0)
            with eng.Fori(1, full) as it:
                for m in range(NX, 2 * NX):
                    step(m, it)
            for m in range(NX * (full + 1), SLOTS + lags):
                step(m, 0)

        def later(j, k, it):
            return j >= k or looped(it)

        CLOSE = SLOTS - 5

        def closing(j, it):
            return not looped(it) and j >= CLOSE

        def wait_rows(eng, r, j, it):
            if closing(j, it):
                eng.wait_ge(s_close[r], j - CLOSE + 1)
            else:
                eng.wait_ge(s_fin[r], j + 1 + NX * it)

        def live(m, lag):
            return 0 <= m - lag < SLOTS

        registers = [0]

        def register_of(eng, at, top):
            registers[0] += 1
            reg = eng.alloc_register(f"loaded{registers[0]}")
            eng.reg_load(reg, at)
            return eng.snap(reg, donate=True, min_val=0, max_val=top)

        def expert(eng, j, it):
            return register_of(eng, ET[0:1, ds(j + NX * it, 1)] if looped(it) else ET[0:1, j:j + 1], E - 1)

        def fill_tails(eng, r, experts_):
            eng.wait_ge(tail_ready[r], 1)
            for e in experts_:
                row = register_of(eng, TAIL[0:1, e:e + 1], E * REGION * P - P)
                eng.dma_start(slots[r][ds(row, P), :], FILL[:, :]).then_inc(tail_filled[r], 16)

        def apart(eng, passed):
            eng.sem_inc(passed, 1)

        @block.sync
        def _(sp):
            def load_x(t0, t1, k):
                sp.dma_start(ROWS[:, t0:t1, 0:D], x_rows[:, t0:t1, :]).then_inc(x_in[k], 16)

            load_x(0, G, 0)
            load_x(G, 2 * G, 1)
            sp.dma_start(CTX[:, :, :], context.rearrange("b m c -> (b m) c").rearrange("(k p) c -> p k c", p=P))\
                .then_inc(attw_in, 16)
            sp.dma_start(WKR[:, :, :], Wk.rearrange("c (h q) -> c h q", h=H)).then_inc(attw_in, 16)
            sp.dma_start(WVR[:, :, :], Wv.rearrange("c (h q) -> c h q", h=H)).then_inc(attw_in, 16)
            sp.dma_start(WQR[:, :, :], Wq.rearrange("d (h q) -> d h q", h=H)).then_inc(attw_in, 16)
            sp.dma_start(WOR[:, :, :], Wout.rearrange("(h p) q -> p h q", h=H)).then_inc(attw_in, 16)
            sp.dma_start(WRAW[:, 0, :], w1[0]).then_inc(w1_in[0], 16)
            load_x(2 * G, T, 2)
            sp.dma_start(WRAW[:, 1:E, :], w1[1:E].rearrange("e d f -> d e f")).then_inc(w1_in[1], 16)
            sp.wait_ge(fill_ready, 1)
            for r in range(2):
                sp.dma_start(slots[r][E * REGION * P:, :].rearrange("(j p) w -> p j w", p=P),
                             FILL[:, :].unsqueeze(1).to_broadcast([P, EMPTY, ROW])).then_inc(slots_filled, 16)
            for e in range(E):
                if e == E - 1:
                    sp.wait_ge(wT_ps, H)
                    sp.dma_start(B1[:, 0:B1_EARLY, :], b1[0:B1_EARLY].partition_broadcast(P)).then_inc(b1_in[0], 16)
                sp.wait_ge(w1_lo, e + 1)
                sp.dma_start(WRAW[:, e, :].rearrange("p (c d) -> p c d", c=FC),
                             w2[e].rearrange("(c p) d -> p c d", p=P)).then_inc(w2_in[e], 16)

            def experts(r):
                if r == 0:
                    sp.wait_ge(ww_ps, H)
                else:
                    sp.wait_ge(pT_hi, UNITS + LAG_AV - LAG_T)
                    sp.wait_ge(pT_lo, UNITS + LAG_AV - LAG_T - 1)
                    sp.wait_ge(av, UNITS)
                if r == 0:
                    fill_tails(sp, r, range(0, E, 2))
                first = B1_EARLY if r == 0 else 0
                sp.dma_start(B1[:, first:E, :], b1[first:E].partition_broadcast(P)).then_inc(b1_in[r], 16)
                if r == 1:
                    fill_tails(sp, r, range(0, E, 2))
                sp.wait_ge(slots_filled, 32)
                sp.wait_ge(routed[r], 1)
                sp.wait_ge(tail_filled[r], 16 * E)
                for k in range(2):
                    sp.wait_ge(sorted_rows[k], 16 * T // 2 * (r + 1))

                slot_tiles = slots[r].rearrange("(j p) w -> p j w", p=P)

                def load(m, it):
                    if not live(m, 0):
                        return
                    at = TB[0:1, ds(m + NX * it, 1)] if looped(it) else TB[0:1, m:m + 1]
                    block_ = register_of(sp, at, E * REGION + EMPTY - 1)
                    if later(m, NX, it):
                        sp.wait_ge(s_x2[r], m - NX + 1 + NX * it)
                        sp.wait_ge(s_ids[r], m - NX + 1 + NX * it)
                    sp.dma_start(XS[:, m % NX:m % NX + 1, :], slot_tiles[:, ds(block_, 1), :])\
                        .then_inc(slot_in[r][m % NX], 16)
                    if m == 1:
                        if r == 0:
                            sp.wait_ge(vw_ps, H)
                        sp.dma_start(B2[:, :, :], b2.partition_broadcast(P)).then_inc(b2_in[r], 16)

                tiles(sp, load, 0)

            experts(0)
            for k in range(NX):
                sp.wait_ge(slot_out[0][k], 16 * ((SLOTS - 1 - k) // NX + 1))
            sp.dma_start(ROWS[:, 0:G, 0:D], x1_rows[:, 0:G, :]).then_inc(x1_in[0], 16)
            sp.dma_start(ROWS[:, G:T, 0:D], x1_rows[:, G:T, :]).then_inc(x1_in[1], 16)
            experts(1)
            for k in range(NX):
                sp.wait_ge(slot_out[1][k], 16 * ((SLOTS - 1 - k) // NX + 1))

        @block.gpsimd
        def _(pool):
            pool.memset(IDN[:, :], 0.0).then_inc(memsets, 1)
            pool.memset(BEFORE[:, :], 0.0).then_inc(memsets, 1)
            pool.memset(FILL[:, :], 0.0).then_inc(memsets, 1)
            pool.memset(ONES[:, :], 1.0)
            pool.memset(NHALF[:, :], -0.5).then_inc(memsets, 1)
            pool.memset(ONF[:, :], 1.0)
            for r in range(2):
                pool.memset(OH[r][0][:, :, 0:1], 0.0)
            pool.wait_ge(memsets, 4)
            pool.affine_select(out=IDN[:, :], in_=IDN[:, :], compare_op=ALU.not_equal, fill=1.0, base=0,
                               pattern=[[-1, P]], channel_multiplier=1)
            pool.affine_select(out=BEFORE[:, :], in_=BEFORE[:, :], compare_op=ALU.is_ge, fill=1.0, base=0,
                               pattern=[[-1, P]], channel_multiplier=1)
            pool.iota(PREF[:, :], pattern=[[-1, E]], base=E, channel_multiplier=0,
                      allow_small_or_imprecise_dtypes=True)
            pool.iota(BASE[:, :, :], pattern=[[REGION, E], [0, G]], base=0, channel_multiplier=0,
                      allow_small_or_imprecise_dtypes=True)
            pool.iota(BASER[:, :], pattern=[[REGION * P, E]], base=0, channel_multiplier=0,
                      allow_small_or_imprecise_dtypes=True)
            pool.iota(TIDX[:, :], pattern=[[1, SLOTS]], base=0, channel_multiplier=0,
                      allow_small_or_imprecise_dtypes=True).then_inc(consts_ready, 1)
            pool.iota(FILL[:, ID:ID + 1].bitcast(i32), pattern=[[0, 1]], base=N, channel_multiplier=0)\
                .then_inc(fill_ready, 1)
            pool.iota(ROWS[:, :, ID].bitcast(i32), pattern=[[1, T]], base=0, channel_multiplier=T)\
                .then_inc(consts_ready, 1)

            def rstd(kind, job):
                pool.wait_ge(ln_ve[kind], job + 1)
                pool.tensor_tensor(RS[kind][:, :], VE[kind][:, :], NHALF[:, :], ALU.pow).then_inc(ln_rstd[kind], 1)

            def sort_tile(r, job, k, i, rows):
                if i == 0:
                    pool.wait_ge(pos_ready, job + 1)
                    pool.wait_ge(ln_keep, job + 1)
                    apart(pool, pool_passed)
                pool.indirect_dma_start(slots[r][:, :], bass.IndirectOffsetOnAxis(ap=POS[k][:, i:i + 1], axis=0),
                                        rows, None).then_inc(sorted_rows[k], 16)

            rstd(GATE, 0)
            rstd(GATE, 1)
            for g in range(NG):
                if g + 2 < NG:
                    rstd(GATE, g + 2)
                for i in range(G):
                    sort_tile(0, g, g % 2, i, ROWS[:, G * g + i, :])

            def experts(r):
                def step(m, it):
                    if live(m, 5):
                        j = m - 5
                        pool.wait_ge(s_xb[r], j + 1 + NX * it)
                        pool.wait_ge(s_ids[r], j + 1 + NX * it)
                        if later(j, NX, it):
                            pool.wait_ge(slot_out[r][j % NX], 16 * (j // NX) + 16 * it)
                        if not closing(j, it):
                            pool.tensor_tensor(RES[:, j % NX, :], XB2[:, j % 2, :], YT[:, j % 2, :], ALU.add)\
                                .then_inc(s_fin[r], 1)
                        wait_rows(pool, r, j, it)
                        apart(pool, pool_passed)
                        pool.indirect_dma_start(
                            ffn_dst[r], bass.IndirectOffsetOnAxis(ap=IDS[:, j % NX:j % NX + 1], axis=0),
                            RES[:, j % NX, :], None, bounds_check=N - 1, oob_is_err=False)\
                            .then_inc(slot_out[r][j % NX], 16)

                tiles(pool, step, 5)

            experts(0)
            rstd(ATT, 0)

            def slot(n, it):
                if n:
                    u = n - 1
                    pool.wait_ge(row_inv, u + 1 + BODY * it)
                    apart(pool, pool_passed)
                    pool.tensor_scalar(PR[:, u % 4, :], PR[:, u % 4, :], RI[:, u % 4:u % 4 + 1], 1.0,
                                       ALU.mult, ALU.mult).then_inc(normed, 1)
                for g in at_step(n, it, 12):
                    rstd(ATT, shifted(g + 1, it))
                for i in range(G):
                    for g in at_step(n, it, 14 + 2 * i, 2):
                        sort_tile(1, shifted(NG + g - 2, it), g % 2, i, X2[g % 2][:, i, :])
                for g in at_step(n, it, 28, 1):
                    rstd(GATE, shifted(NG + g - 1, it))

            rounds(pool, slot)
            rstd(GATE, 2 * NG - 1)
            for i in range(G):
                sort_tile(1, 2 * NG - 2, 0, i, X2[0][:, i, :])
            for i in range(G):
                sort_tile(1, 2 * NG - 1, 1, i, X2[1][:, i, :])
            experts(1)

        @block.scalar
        def _(act):
            act.dma_start(GWR[:, :], gate_w).then_inc(small_in, 16)
            act.dma_start(GB[:, :], gate_b.partition_broadcast(P)).then_inc(small_in, 16)
            act.dma_start(EB[:, :], expert_bias.partition_broadcast(P)).then_inc(small_in, 16)
            act.dma_start(BO[:, :], bout.rearrange("(d a) -> d a", a=1)).then_inc(small_in, 16)

            def norm(kind, job, rows, tiles_):
                act.wait_ge(ln_shift[kind], job + 1)
                if kind == ATT:
                    act.wait_ge(ln_T[GATE], job + NG - 2 if looped(job) or job >= 2 else NG)
                elif looped(job) or job >= NG:
                    act.wait_ge(ln_T[ATT], job - NG + 3 if looped(job) or job < 2 * NG - 1 else NG + 1)
                elif job:
                    act.wait_ge(ln_T[GATE], job)
                for i in tiles_:
                    last = act.activation(XN[:, i, :], rows(i), ACT.Identity, bias=SH[kind][:, i:i + 1],
                                          scale=RS[kind][:, i:i + 1])
                if i == G - 1:
                    last.then_inc(ln_xn[kind], 1)

            def rows_at(t0):
                return lambda i: (ROWS[:, t0 + i, 0:D] if isinstance(t0, int) else
                                  ROWS[:, ds(t0 + i, 1), 0:D].rearrange("p a d -> p (a d)"))

            def x2_at(k):
                return lambda i: X2[k][:, i, 0:D]

            def raw_evac(job, bank):
                act.wait_ge(ln_T[GATE], job + 1)
                if isinstance(job, int) and job < NG:
                    if job:
                        act.wait_ge(logit_ps, job)
                else:
                    act.wait_ge(oT_ps, job - NG + 1)
                act.activation(XNT[:, :], BK[bank][:, :], ACT.Copy).then_inc(raw_T, 1)

            def wT_evac(h):
                act.wait_ge(wT_ps, h + 1)
                if h:
                    act.wait_ge(ww_ps, h)
                act.activation(WT[:, :], BK[0][:, 0:P + 2 * C], ACT.Copy).then_inc(wT_ready, 1)

            def ww_evac(h):
                act.wait_ge(ww_ps, h + 1)
                if h:
                    act.wait_ge(m_ps, h)
                    act.wait_ge(vw_ps, h)
                act.activation(WW[:, :, :].rearrange("c s d -> c (s d)"), BK[1][0:C, 0:2 * D], ACT.Copy)\
                    .then_inc(ww_ready, 1)

            def products(h):
                act.wait_ge(m_ps, h + 1)
                act.activation(MH[:, h, :], BK[2 + h % 2][:, :], ACT.Copy).then_inc(m_hi, 1)
                act.wait_ge(vw_ps, h + 1)
                act.activation(VWH[:, h, :, :].rearrange("p c d -> p (c d)"), BK[4][:, :], ACT.Copy)\
                    .then_inc(vw_hi, 1)

            def w2_high(e):
                act.wait_ge(w2_in[e], 16)
                act.activation(W2HL[:, e, :, 0, :], WRAW[:, e, :].rearrange("p (c d) -> p c d", c=FC), ACT.Copy)\
                    .then_inc(w2_hi, 1)

            act.wait_ge(x_in[0], 16)
            norm(GATE, 0, rows_at(0), range(G))
            raw_evac(0, 6)
            act.wait_ge(ctxT_ps, 1)
            act.activation(CTXT[:, :], BK[5][0:C, :], ACT.Copy, accum_out=CM[:, 0:1]).then_inc(ctxT_ready, 1)
            act.wait_ge(ctx_mean, 1)
            act.activation(CTXK[:, :], CTXT[:, :], ACT.Identity, bias=CM[:, 1:2], scale=SHARPEN * SCALE)\
                .then_inc(ctxK_ready, 1)
            wT_evac(0)
            ww_evac(0)
            wT_evac(1)
            for s in range(NG + LAG_W2):
                h = s
                if s + 1 < NG:
                    act.wait_ge(x_in[min(s + 1, 2)], 16)
                    norm(GATE, s + 1, rows_at(G * (s + 1)), range(G))
                if h < H:
                    products(h)
                if s == NG:
                    fill_tails(act, 0, range(1, E, 2))
                if h < H - 1:
                    ww_evac(h + 1)
                if s + 1 < NG:
                    raw_evac(s + 1, 6)
                if h < H - 2:
                    wT_evac(h + 2)
                if s < E:
                    act.wait_ge(w1_in[min(s, 1)], 16)
                    act.activation(W1H[:, s, :], WRAW[:, s, :], ACT.Copy).then_inc(w1_hi, 1)
                if 0 <= s - LAG_W2 < E:
                    w2_high(s - LAG_W2)

            def experts(r):
                def slot_norm(m, it):
                    act.wait_ge(slot_in[r][m % NX], 16 * (m // NX + 1) + 16 * it)
                    if later(m, 2, it):
                        act.wait_ge(s_xT[r], m - 1 + NX * it)
                    act.activation(XSN[:, m % 2, :], XS[:, m % NX, 0:D], ACT.Identity,
                                   bias=XS[:, m % NX, SHIFT:SHIFT + 1], scale=XS[:, m % NX, RSTD:RSTD + 1])\
                        .then_inc(s_xn[r], 1)

                def step(m, it):
                    if live(m, 5):
                        j = m - 5
                        act.wait_ge(s_y[r], j + 1 + NX * it)
                        if later(j, 2, it):
                            wait_rows(act, r, j - 2, it)
                        act.activation(YT[:, j % 2, :], BK[6 + j % 2][:, D:2 * D], ACT.Copy, scale=0.5)\
                            .then_inc(s_yb[r], 1)
                    if live(m, 3):
                        j = m - 3
                        act.wait_ge(s_hT[r], j + 1 + NX * it)
                        if later(j, 2, it):
                            act.wait_ge(s_y[r], j - 1 + NX * it)
                        act.activation(HTH[:, j % 2, :], BK[4 + j % 2][:, :], ACT.Relu).then_inc(s_hhi[r], 1)
                    if live(m, 0):
                        if m == 0 and r == 0:
                            act.wait_ge(w2_lo, E)
                        act.wait_ge(s_xT[r], m + 1 + NX * it)
                        if later(m, 2, it):
                            act.wait_ge(s_h[r], m - 1 + NX * it)
                        act.activation(XTH[:, m % 2, :], BK[m % 2][:, 0:P], ACT.Copy).then_inc(s_xhi[r], 1)
                    if live(m, -1):
                        slot_norm(m + 1, it)

                if r == 1:
                    fill_tails(act, r, range(1, E, 2))
                slot_norm(0, 0)
                tiles(act, step, 5)

            experts(0)

            act.wait_ge(x1_in[0], 16)
            norm(ATT, 0, rows_at(0), range(G // 2, G))

            def xT_evac(g, it):
                act.wait_ge(ln_T[ATT], shifted(g, it) + 1)
                act.activation(AXH[:, g % 2, :], BK[6][:, :], ACT.Copy).then_inc(xT_hi, 1)

            xT_evac(0, 0)

            def slot(n, it):
                act.wait_ge(neg_max, n + 1 + BODY * it)
                if n >= 4:
                    act.wait_ge(pT_ps, n - 3 + BODY * it)
                act.activation(PR[:, n % 4, :], BK[n % 2][:, :], ACT.Exp, bias=NM[:, n % 4:n % 4 + 1],
                               accum_out=SU[:, n % 4:n % 4 + 1]).then_inc(probs, 1)
                if n >= LAG_T:
                    u = n - LAG_T
                    act.wait_ge(pT_ps, u + 1 + BODY * it)
                    if u % G == 0 and (u // G >= 2 or looped(it)):
                        act.wait_ge(av, G * (u // G) - G + BODY * it)
                    act.activation(PTH[:, (u // G) % 2, :, (u % G) * P:(u % G + 1) * P],
                                   BK[2 + u % 2][:, :].rearrange("p (c q) -> p c q", c=KC), ACT.Copy)\
                        .then_inc(pT_hi, 1)
                for i in range(G):
                    for g in at_step(n, it, 14 + i):
                        norm(ATT, shifted(g + 1, it), rows_at(group_tile(g + 1, it)), [i])
                for g in at_step(n, it, 20):
                    xT_evac(g + 1, it)
                for g in at_step(n, it, 8, 1):
                    o_evac(g - 1, it)
                for i in range(2):
                    for g in at_step(n, it, 30 + i, 1):
                        norm(GATE, shifted(NG + g - 1, it), x2_at((g - 1) % 2), [i])
                    for g in at_step(n, it, i, 2):
                        norm(GATE, shifted(NG + g - 2, it), x2_at(g % 2), [2 + i])
                for g in at_step(n, it, 3, 2):
                    raw_evac(shifted(NG + g - 2, it), 7)

            def o_evac(g, it):
                act.wait_ge(av, HG * (g + 1) + BODY * it)
                act.wait_ge(logit_ps, NG + g + 2 * it)
                act.activation(XNT[:, :], BK[4 + g % 2][:, :], ACT.Identity, bias=BO[:, 0:1]).then_inc(o_kept, 1)

            rounds(act, slot)
            o_evac(NG - 1, 0)
            norm(GATE, 2 * NG - 1, x2_at(1), range(G // 2, G))
            raw_evac(2 * NG - 1, 7)
            experts(1)

        @block.vector
        def _(dve):
            v = nc.vector

            def row_of(t):
                return ROWS[:, t, 0:D] if isinstance(t, int) else ROWS[:, ds(t, 1), 0:D].rearrange("p a d -> p (a d)")

            def rows_at(t0):
                return lambda i: row_of(t0 + i)

            def x2_at(k):
                return lambda i: X2[k][:, i, 0:D]

            def stats(kind, job, rows, tiles_):
                if looped(job):
                    apart(dve, dve_passed)
                for i in tiles_:
                    last = v.bn_stats(BN[kind][:, i, :], rows(i))
                if i == G - 1:
                    last.then_inc(ln_bn[kind], 1)

            def moments(kind, job):
                dve.wait_ge(ln_bn[kind], job + 1)
                if looped(job) or job:
                    dve.wait_ge(ln_xn[kind], job)
                apart(dve, dve_passed)
                for i in range(G):
                    last = v.bn_aggr(MV[kind][:, i, :], BN[kind][:, i, :])
                last.then_inc(ln_agg[kind], 1)
                dve.wait_ge(ln_agg[kind], job + 1)
                v.tensor_scalar(VE[kind][:, :], MV[kind][:, :, 1], EPS, None, ALU.add).then_inc(ln_ve[kind], 1)

            def shift(kind, job, span=None, t0=None):
                dve.wait_ge(ln_rstd[kind], job + 1)
                v.scalar_tensor_tensor(out=SH[kind][:, :], in0=MV[kind][:, :, 0], scalar=-1.0, in1=RS[kind][:, :],
                                       op0=ALU.mult, op1=ALU.mult).then_inc(ln_shift[kind], 1)
                if kind == GATE:
                    dve.wait_ge(ln_shift[kind], job + 1)
                    v.tensor_copy(span[:, :, SHIFT:SHIFT + 1], SH[kind][:, :].unsqueeze(2))
                    if t0 is not None:
                        ids = ROWS[:, t0:t0 + G, ID:ID + 1] if isinstance(t0, int) else ROWS[:, ds(t0, G), ID:ID + 1]
                        v.tensor_copy(span[:, :, ID:ID + 1].bitcast(i32), ids.bitcast(i32))
                    v.tensor_copy(span[:, :, RSTD:RSTD + 1], RS[kind][:, :].unsqueeze(2)).then_inc(ln_keep, 1)

            def norm_first(kind, rows):
                for i in range(G // 2):
                    last = v.tensor_scalar(XN[:, i, :], rows(i), RS[kind][:, i:i + 1], SH[kind][:, i:i + 1],
                                           ALU.mult, ALU.add)
                last.then_inc(xn_first, 1)

            CHAIN = 6

            def onehot(r, job, k, steps):
                bias = lambda b: b[:, :].unsqueeze(1).to_broadcast([P, G, E])
                over = lambda: MX[:, :].unsqueeze(2).to_broadcast([P, G, E])
                lg = LG[:, :, :]
                mine = OH[r][k]
                for i in steps:
                    if i == 0:
                        dve.wait_ge(logit_ps, job + 1)
                    elif i < 7:
                        dve.wait_ge(onehot_step, CHAIN * job + i)
                    if i == 0:
                        v.tensor_tensor(lg, BK[7][:, 0:G * E].rearrange("p (t e) -> p t e", e=E), bias(GB), ALU.add)\
                            .then_inc(onehot_step, 1)
                    elif i == 1:
                        v.tensor_tensor(lg, lg, bias(EB), ALU.add).then_inc(onehot_step, 1)
                    elif i == 2:
                        v.tensor_reduce(MX[:, :], lg, AX.X, ALU.max).then_inc(onehot_step, 1)
                    elif i == 3:
                        v.tensor_tensor(lg, lg, over(), ALU.is_ge).then_inc(onehot_step, 1)
                    elif i == 4:
                        v.tensor_tensor(lg, lg, bias(PREF), ALU.mult).then_inc(onehot_step, 1)
                    elif i == 5:
                        v.tensor_reduce(MX[:, :], lg, AX.X, ALU.max).then_inc(onehot_step, 1)
                    elif i == 6:
                        v.tensor_tensor(mine[:, :, 1:1 + G].rearrange("p e t -> p t e"), lg, over(), ALU.is_equal)\
                            .then_inc(onehot_ready, 1)
                    elif i == 7:
                        dve.wait_ge(onehot_ready, job + 1)
                        with nc.allow_low_precision(reason="whole numbers up to T are exact"):
                            v.tensor_reduce(OH[r][1 - k][:, :, 0], mine[:, :, :], AX.X, ALU.add)\
                                .then_inc(sum_ready, 1)

            def positions(r, job, k, earlier, steps):
                for i in steps:
                    if i == 0:
                        dve.wait_ge(rank_ps, job + 1)
                        counted = BK[RANK_BANK[r]][:, RANKS:RANKS + E * G].rearrange("p (e t) -> p e t", e=E)
                        v.tensor_tensor(WRK[:, :, :], counted, OH[r][k][:, :, 1:1 + G], ALU.mult).then_inc(ranked, 1)
                    elif i == 1:
                        dve.wait_ge(ranked, job + 1)
                        v.tensor_reduce(POSF[:, :], WRK[:, :, :].rearrange("p e t -> p t e"), AX.X, ALU.add)\
                            .then_inc(pos_step, 1)
                    else:
                        dve.wait_ge(pos_step, job + 1)
                        if looped(earlier) or earlier:
                            dve.wait_ge(sorted_rows[k], 16 * G * earlier)
                        v.tensor_copy(POS[k][:, :], POSF[:, :]).then_inc(pos_ready, 1)

            def table(r):
                step = [0]

                def link(ins):
                    step[0] += 1
                    ins.then_inc(table_step[r], 1)
                    dve.wait_ge(table_step[r], step[0])

                dve.wait_ge(total_ps[r], 1)
                total = BK[RANK_BANK[r]][:, TOTALS:TOTALS + E]
                tiles_of, ends, skip = (CNT[:, i, :] for i in range(3))
                per_tile = lambda a: a.unsqueeze(1).to_broadcast([P, SLOTS, E])
                v.tensor_tensor(TAIL[:, :], total, BASER[:, :], ALU.add).then_inc(tail_ready[r], 1)
                link(v.tensor_scalar(CNTI[:, 0, :], total, float(P - 1), None, ALU.add))
                link(v.tensor_scalar(CNTI[:, 1, :], CNTI[:, 0, :], 7, None, ALU.arith_shift_right))
                link(v.tensor_copy(tiles_of, CNTI[:, 1, :]))
                link(v.tensor_tensor_scan(ends, ONF[:, 0:1].to_broadcast([P, E]), tiles_of, 0.0, ALU.mult, ALU.add))
                link(v.tensor_scalar(skip, tiles_of, -1.0, float(REGION), ALU.mult, ALU.add))
                link(v.tensor_tensor(SEL[:, :, :], per_tile(ends), TIDX[:, :].unsqueeze(2).to_broadcast([P, SLOTS, E]),
                                     ALU.is_le))
                link(v.tensor_reduce(ETF[:, :], SEL[:, :, :], AX.X, ALU.add))
                link(v.tensor_scalar(ET[:, :], ETF[:, :], float(E - 1), None, ALU.min))
                link(v.tensor_tensor(SEL[:, :, :], SEL[:, :, :], per_tile(skip), ALU.mult))
                link(v.tensor_reduce(ETF[:, :], SEL[:, :, :], AX.X, ALU.add))
                v.tensor_tensor(TB[:, :], ETF[:, :], TIDX[:, :], ALU.add).then_inc(routed[r], 1)

            def experts(r):

                def step(m, it):
                    if m == 2:
                        dve.wait_ge(b2_in[r], 16)
                        v.tensor_scalar(B2[:, :, :], B2[:, :, :], 0.5, None, ALU.mult).then_inc(bias_half[r], 1)
                        dve.wait_ge(bias_half[r], 1)
                        dve.wait_ge(b1_in[r], 16 * (2 - r))
                    if live(m, 2):
                        j = m - 2
                        e = expert(dve, j, it)
                        dve.wait_ge(s_h[r], j + 1 + NX * it)
                        if later(j, 3, it):
                            dve.wait_ge(s_hT[r], j - 2 + NX * it)
                        v.tensor_tensor(HB[:, j % 3, :].unsqueeze(1), BK[2 + j % 2][:, :].unsqueeze(1),
                                        B1[:, ds(e, 1), :], ALU.add).then_inc(s_hb[r], 1)
                        if later(j, NX, it):
                            dve.wait_ge(s_xb[r], j - NX + 1 + NX * it)
                        v.tensor_tensor(XB[:, j % NX, :].unsqueeze(1), XS[:, j % NX, 0:D].unsqueeze(1),
                                        B2[:, ds(e, 1), :], ALU.add).then_inc(s_x2[r], 1)
                    if live(m, 5):
                        j = m - 5
                        dve.wait_ge(s_yb[r], j + 1 + NX * it)
                        dve.wait_ge(s_x2[r], j + 1 + NX * it)
                        v.scalar_tensor_tensor(out=XB2[:, j % 2, :], in0=BK[6 + j % 2][:, 0:D], scalar=0.5,
                                               in1=XB[:, j % NX, :], op0=ALU.mult, op1=ALU.add).then_inc(s_xb[r], 1)
                        if closing(j, it):
                            dve.wait_ge(s_xb[r], j + 1)
                            dve.wait_ge(slot_out[r][j % NX], 16 * (j // NX))
                            v.tensor_tensor(RES[:, j % NX, :], XB2[:, j % 2, :], YT[:, j % 2, :], ALU.add)\
                                .then_inc(s_close[r], 1)
                    if live(m, 3):
                        j = m - 3
                        dve.wait_ge(s_hhi[r], j + 1 + NX * it)
                        v.scalar_tensor_tensor(out=HTL[:, j % 2, :], in0=BK[4 + j % 2][:, :], scalar=0.0,
                                               in1=HTH[:, j % 2, :].bitcast(fp32), op0=ALU.max,
                                               op1=ALU.subtract).then_inc(s_hlo[r], 1)
                    if live(m, 0):
                        dve.wait_ge(s_xhi[r], m + 1 + NX * it)
                        v.tensor_tensor(XTL[:, m % 2, :], BK[m % 2][:, 0:P], XTH[:, m % 2, :].bitcast(fp32),
                                        ALU.subtract).then_inc(s_xlo[r], 1)
                    if live(m, 2):
                        j = m - 2
                        dve.wait_ge(slot_in[r][j % NX], 16 * (j // NX + 1) + 16 * it)
                        if later(j, NX, it):
                            dve.wait_ge(slot_out[r][j % NX], 16 * (j // NX) + 16 * it)
                        v.tensor_copy(IDS[:, j % NX:j % NX + 1], XS[:, j % NX, ID:ID + 1].bitcast(i32))\
                            .then_inc(s_ids[r], 1)

                tiles(dve, step, 5)

            def w1_low(e):
                dve.wait_ge(w1_hi, e + 1)
                v.tensor_tensor(W1L[:, e, :], WRAW[:, e, :], W1H[:, e, :].bitcast(fp32), ALU.subtract)\
                    .then_inc(w1_lo, 1)

            def w2_low(e):
                dve.wait_ge(w2_hi, e + 1)
                v.tensor_tensor(W2HL[:, e, :, 1, :], WRAW[:, e, :].rearrange("p (c d) -> p c d", c=FC),
                                W2HL[:, e, :, 0, :].bitcast(fp32), ALU.subtract).then_inc(w2_lo, 1)

            def head(h):
                dve.wait_ge(m_hi, h + 1)
                v.tensor_tensor(ML[:, h, :], BK[2 + h % 2][:, :], MH[:, h, :].bitcast(fp32), ALU.subtract)\
                    .then_inc(m_lo, 1)
                dve.wait_ge(vw_hi, h + 1)
                v.tensor_tensor(VWL[:, h, :, :].rearrange("p c d -> p (c d)"), BK[4][:, :],
                                VWH[:, h, :, :].rearrange("p c d -> p (c d)").bitcast(fp32), ALU.subtract)\
                    .then_inc(vw_lo, 1)

            def ln_start(g):
                dve.wait_ge(x_in[min(g, 2)], 16)
                stats(GATE, g, rows_at(G * g), range(G))
                moments(GATE, g)

            def ln_end(g):
                shift(GATE, g, ROWS[:, G * g:G * g + G, :])

            ln_start(0)
            dve.wait_ge(consts_ready, 2)
            ln_end(0)
            ln_start(1)
            dve.wait_ge(gate_ps, 1)
            v.tensor_copy(GWT[:, :], BK[5][:, 0:E]).then_inc(gate_ready, 1)
            ln_end(1)
            dve.wait_ge(small_in, 64)
            onehot(0, 0, 0, range(8))
            dve.wait_ge(ctxT_ready, 1)
            v.tensor_scalar(CM[:, 1:2], CM[:, 0:1], -(SHARPEN - 1.0) * SCALE / KEYS, None, ALU.mult)\
                .then_inc(ctx_mean, 1)
            positions(0, 0, 0, 0, range(3))
            ln_start(2)
            ln_end(2)
            for s in range(NG + LAG_W2):
                if 0 < s < NG:
                    for i in range(8):
                        onehot(0, s, s % 2, [i])
                        if s + 2 < NG and i < G:
                            stats(GATE, s + 2, rows_at(G * (s + 2)), [i])
                        elif s + 2 < NG and i == 6:
                            moments(GATE, s + 2)
                if s == NG:
                    table(0)
                if s < H:
                    head(s)
                if 0 < s < NG:
                    positions(0, s, s % 2, s // 2, range(3))
                    if s + 2 < NG:
                        ln_end(s + 2)
                if s < E:
                    w1_low(s)
                if 0 <= s - LAG_W2 < E:
                    w2_low(s - LAG_W2)

            experts(0)

            def xT_low(g, it, cols):
                dve.wait_ge(xT_hi, g + 1 + 2 * it)
                last = v.tensor_tensor(AXL[:, g % 2, cols], BK[6][:, cols], AXH[:, g % 2, cols].bitcast(fp32),
                                       ALU.subtract)
                if cols.stop == G * P:
                    last.then_inc(xT_lo, 1)

            dve.wait_ge(x1_in[0], 16)
            stats(ATT, 0, rows_at(0), range(G))
            moments(ATT, 0)
            shift(ATT, 0)
            dve.wait_ge(ln_shift[ATT], 1)
            dve.wait_ge(ln_T[GATE], NG)
            norm_first(ATT, rows_at(0))
            xT_low(0, 0, slice(0, G * P))

            def new_rows(g, it, i):
                dve.wait_ge(oT_ps, g + 1 + 2 * it)
                dve.wait_ge(sorted_rows[g % 2], 16 * G * ((NG + g) // 2 + it))
                v.tensor_tensor(X2[g % 2][:, i, 0:D], row_of(group_tile(g, it) + i), BK[7][:, i * D:(i + 1) * D],
                                ALU.add).then_inc(x2_ready, 1)

            def slot(n, it):
                dve.wait_ge(scores, n + 1 + BODY * it)
                v.tensor_reduce(NM[:, n % 4:n % 4 + 1], BK[n % 2][:, :], AX.X, ALU.max, negate=True)\
                    .then_inc(neg_max, 1)
                if n >= LAG_T + 1:
                    u = n - LAG_T - 1
                    dve.wait_ge(pT_hi, u + 1 + BODY * it)
                    at = (slice(None), (u // G) % 2, slice(None), slice((u % G) * P, (u % G + 1) * P))
                    v.tensor_tensor(PTL[at], BK[2 + u % 2][:, :].rearrange("p (c q) -> p c q", c=KC),
                                    PTH[at].bitcast(fp32), ALU.subtract).then_inc(pT_lo, 1)
                if n:
                    u = n - 1
                    dve.wait_ge(probs, u + 1 + BODY * it)
                    v.reciprocal(RI[:, u % 4:u % 4 + 1], SU[:, u % 4:u % 4 + 1]).then_inc(row_inv, 1)
                for i in range(G):
                    for g in at_step(n, it, 7 + i):
                        if n == 7 and not looped(it):
                            dve.wait_ge(x1_in[1], 16)
                        stats(ATT, shifted(g + 1, it), rows_at(group_tile(g + 1, it)), [i])
                for g in at_step(n, it, 11):
                    moments(ATT, shifted(g + 1, it))
                for g in at_step(n, it, 13):
                    shift(ATT, shifted(g + 1, it))
                for half in range(2):
                    for g in at_step(n, it, 21 + half):
                        xT_low(g + 1, it, slice(half * 2 * P, (half + 1) * 2 * P))
                for i in range(G):
                    for g in at_step(n, it, 15 + i, 1):
                        new_rows(g - 1, it, i)
                for i in range(G):
                    for g in at_step(n, it, 23 + i, 1):
                        dve.wait_ge(x2_ready, G * shifted(g - 1, it) + i + 1)
                        stats(GATE, shifted(NG + g - 1, it), x2_at((g - 1) % 2), [i])
                for g in at_step(n, it, 27, 1):
                    moments(GATE, shifted(NG + g - 1, it))
                for g in at_step(n, it, 29, 1):
                    shift(GATE, shifted(NG + g - 1, it), X2[(g - 1) % 2][:, :, :], group_tile(g - 1, it))
                for i in range(3):
                    for g in at_step(n, it, 5 + i, 2):
                        onehot(1, shifted(NG + g - 2, it), g % 2, range(3 * i, min(3 * i + 3, 8)))
                for i in range(3):
                    for g in at_step(n, it, 11 + i, 2):
                        positions(1, shifted(NG + g - 2, it), g % 2, shifted((NG + g - 2) // 2, it, 1), [i])

            rounds(dve, slot)
            positions(1, 2 * NG - 2, 0, NG - 1, range(3))
            for i in range(G):
                new_rows(NG - 1, 0, i)
            dve.wait_ge(x2_ready, T)
            stats(GATE, 2 * NG - 1, x2_at(1), range(G))
            moments(GATE, 2 * NG - 1)
            shift(GATE, 2 * NG - 1, X2[1][:, :, :], T - G)
            dve.wait_ge(ln_T[ATT], NG + 1)
            norm_first(GATE, x2_at(1))
            onehot(1, 2 * NG - 1, 1, range(8))
            positions(1, 2 * NG - 1, 1, NG - 1, range(3))
            table(1)
            experts(1)

        @block.tensor
        def _(pe):
            def xn_transposes(kind, job, bank):
                pe.wait_ge(ln_xn[kind], job + 1)
                for i in range(G):
                    last = pe.transpose(BK[bank][:, i * P:(i + 1) * P], XN[:, i, :], IDN[:, :])
                last.then_inc(ln_T[kind], 1)

            def gate_logits(job):
                pe.wait_ge(raw_T, job + 1)
                for i in range(G):
                    last = pe.matmul(BK[7][:, i * E:(i + 1) * E], XNT[:, i * P:(i + 1) * P], GWT[:, :],
                                     start=True, stop=True)
                last.then_inc(logit_ps, 1)

            def ranks(r, job, k):
                pe.wait_ge(onehot_ready, job + 1)
                if looped(job) or job:
                    pe.wait_ge(sum_ready, job)
                    pe.wait_ge(ranked, job)
                out = BK[RANK_BANK[r]][:, RANKS:RANKS + E * G].rearrange("p (e t) -> p e t", e=E)
                mine = OH[r][k]
                pe.matmul(out, ONES[:, :], BASE[:, :, :], start=True, stop=False)
                for i in range(G):
                    pe.matmul(out[:, :, i:G], ONES[:, :], mine[:, :, i:i + 1].to_broadcast([P, E, G - i]),
                              start=False, stop=False)
                pe.matmul(out, BEFORE[:, :], mine[:, :, 1:1 + G], start=False, stop=True).then_inc(rank_ps, 1)

            def totals(r):
                pe.wait_ge(sum_ready, NG * (r + 1))
                pe.wait_ge(ranked, NG * (r + 1))
                pe.matmul(BK[RANK_BANK[r]][:, TOTALS:TOTALS + E], ONES[:, :], OH[r][0][:, :, 0], start=True, stop=True)\
                    .then_inc(total_ps[r], 1)

            def three(out, wh, wl, mh, ml, start, stop):
                pe.matmul(out, wh, mh, start=start, stop=False)
                pe.matmul(out, wh, ml, start=False, stop=False)
                return pe.matmul(out, wl, mh, start=False, stop=stop)

            def experts(r):
                def step(m, it):
                    if live(m, 1):
                        e1 = expert(pe, m - 1, it)
                    if live(m, 3):
                        j = m - 3
                        pe.wait_ge(s_hb[r], j + 1 + NX * it)
                        for c in range(FC):
                            last = pe.transpose(BK[4 + j % 2][:, c * P:(c + 1) * P], HB[:, j % 3, c * P:(c + 1) * P],
                                                IDN[:, :])
                        last.then_inc(s_hT[r], 1)
                    if m == 4 and r == 0:
                        pe.wait_ge(w2_lo, E)
                    if live(m, 4):
                        j = m - 4
                        e = expert(pe, j, it)
                        pe.wait_ge(s_hlo[r], j + 1 + NX * it)
                        if later(j, 2, it):
                            pe.wait_ge(s_xb[r], j - 1 + NX * it)
                        for c in range(FC):
                            pe.matmul(BK[6 + j % 2][:, 0:2 * D].rearrange("p (a s d) -> p a s d", a=1, s=2),
                                      HTH[:, j % 2, c * P:(c + 1) * P], W2HL[:, ds(e, 1), c, :, :],
                                      start=(c == 0), stop=False)
                            last = pe.matmul(BK[6 + j % 2][:, 0:D].unsqueeze(1), HTL[:, j % 2, c * P:(c + 1) * P],
                                             W2HL[:, ds(e, 1), c, 0, :], start=False, stop=(c == FC - 1))
                        last.then_inc(s_y[r], 1)
                    if live(m, 0):
                        pe.wait_ge(s_xn[r], m + 1 + NX * it)
                        pe.transpose(BK[m % 2][:, 0:P], XSN[:, m % 2, :], IDN[:, :]).then_inc(s_xT[r], 1)
                    if live(m, 1):
                        j = m - 1
                        pe.wait_ge(s_xlo[r], j + 1 + NX * it)
                        three(BK[2 + j % 2][:, :].unsqueeze(1), XTH[:, j % 2, :], XTL[:, j % 2, :],
                              W1H[:, ds(e1, 1), :], W1L[:, ds(e1, 1), :], True, True).then_inc(s_h[r], 1)

                tiles(pe, step, 4)

            pe.wait_ge(consts_ready, 2)
            pe.wait_ge(small_in, 64)
            pe.transpose(BK[5][:, 0:E], GWR[:, :], IDN[0:E, 0:E]).then_inc(gate_ps, 1)
            xn_transposes(GATE, 0, 6)
            pe.wait_ge(gate_ready, 1)
            gate_logits(0)
            pe.wait_ge(attw_in, 16 * 5)
            for c in range(KC):
                last = pe.transpose(BK[5][0:C, c * P:(c + 1) * P], CTX[:, c, :], IDN[:, :])
            last.then_inc(ctxT_ps, 1)
            pe.wait_ge(ctxT_ready, 1)

            def head_transposes(h):
                if h:
                    pe.wait_ge(wT_ready, h)
                pe.transpose(BK[0][:, 0:P], WQR[:, h, :], IDN[:, :])
                pe.transpose(BK[0][:, P:P + C], WKR[:, h, :], IDN[0:C, 0:C])
                pe.transpose(BK[0][:, P + C:P + 2 * C], WVR[:, h, :], IDN[0:C, 0:C]).then_inc(wT_ps, 1)

            def head_weights(h):
                pe.wait_ge(wT_ready, h + 1)
                if h:
                    pe.wait_ge(ww_ready, h)
                pe.matmul(BK[1][0:C, 0:D], WT[:, P:P + C], WT[:, 0:P], start=True, stop=True)
                pe.matmul(BK[1][0:C, D:2 * D], WT[:, P + C:P + 2 * C], WOR[:, h, :], start=True, stop=True)\
                    .then_inc(ww_ps, 1)

            def head_products(h):
                pe.wait_ge(ww_ready, h + 1)
                if h >= 2:
                    pe.wait_ge(m_lo, h - 1)
                pe.matmul(BK[2 + h % 2][:, :], WW[:, 0, :], CTXK[:, :], start=True, stop=True).then_inc(m_ps, 1)
                if h:
                    pe.wait_ge(vw_lo, h)
                for c in range(KC):
                    last = pe.matmul(BK[4][:, c * D:(c + 1) * D], CTXT[:, c * P:(c + 1) * P], WW[:, 1, :],
                                     start=True, stop=True)
                last.then_inc(vw_ps, 1)

            head_transposes(0)
            head_weights(0)
            ranks(0, 0, 0)
            head_transposes(1)
            pe.wait_ge(ctxK_ready, 1)
            for s in range(NG):
                h = s
                head_products(h)
                if h < H - 1:
                    head_weights(h + 1)
                if s + 1 < NG:
                    pe.wait_ge(raw_T, s + 1)
                    xn_transposes(GATE, s + 1, 6)
                if h < H - 2:
                    head_transposes(h + 2)
                if 0 < s < NG:
                    ranks(0, s, s % 2)
                if s + 1 < NG:
                    pe.wait_ge(onehot_ready, s + 1)
                    gate_logits(s + 1)
                if s == NG - 1:
                    totals(0)

            pe.wait_ge(w1_lo, E)
            pe.wait_ge(vw_lo, H)
            pe.wait_ge(routed[0], 1)
            experts(0)

            wait_rows(pe, 0, SLOTS - 1, 0)
            pe.wait_ge(xn_first, 1)
            xn_transposes(ATT, 0, 6)

            def slot(n, it):
                g = n // HG
                u = n
                h = (u // G) % H
                i = u % G
                if u % HG == 0:
                    pe.wait_ge(xT_lo, g + 1 + 2 * it)
                if u >= 2:
                    pe.wait_ge(probs, u - 1 + BODY * it)
                cols = slice(i * P, (i + 1) * P)
                three(BK[u % 2][:, :], AXH[:, g % 2, cols], AXL[:, g % 2, cols], MH[:, h, :], ML[:, h, :],
                      True, True).then_inc(scores, 1)
                if n >= LAG_AV:
                    u = n - LAG_AV
                    g, h, c = u // HG, (u // G) % H, u % G
                    hh = u // G
                    if c == 0:
                        pe.wait_ge(pT_lo, G * hh + G + BODY * it)
                        if h == 0 and (g >= 2 or looped(it)):
                            pe.wait_ge(o_kept, g - 1 + 2 * it)
                    three(BK[4 + g % 2][:, :], VWH[:, h, c, :], VWL[:, h, c, :], PTH[:, hh % 2, c, :],
                          PTL[:, hh % 2, c, :], h == 0 and c == 0, h == H - 1 and c == KC - 1).then_inc(av, 1)
                if n >= LAG_T:
                    u = n - LAG_T
                    pe.wait_ge(normed, u + 1 + BODY * it)
                    if u >= 2:
                        pe.wait_ge(pT_lo, u - 1 + BODY * it)
                    for c in range(KC):
                        last = pe.transpose(BK[2 + u % 2][:, c * P:(c + 1) * P], PR[:, u % 4, c * P:(c + 1) * P],
                                            IDN[:, :])
                    last.then_inc(pT_ps, 1)
                for g in at_step(n, it, 19):
                    pe.wait_ge(xT_lo, g + 1 + 2 * it)
                    xn_transposes(ATT, shifted(g + 1, it), 6)
                for g in at_step(n, it, 14, 1):
                    o_transposes(g - 1, it)
                for g in at_step(n, it, 2, 2):
                    xn_transposes(GATE, shifted(NG + g - 2, it), 7)
                for g in at_step(n, it, 4, 2):
                    gate_logits(shifted(NG + g - 2, it))
                for g in at_step(n, it, 10, 2):
                    ranks(1, shifted(NG + g - 2, it), g % 2)

            def o_transposes(g, it):
                pe.wait_ge(o_kept, g + 1 + 2 * it)
                pe.wait_ge(onehot_ready, NG + g + 2 * it)
                pe.wait_ge(ranked, NG + g + 2 * it)
                for i in range(G):
                    last = pe.transpose(BK[7][:, i * D:(i + 1) * D], XNT[:, i * P:(i + 1) * P], IDN[:, :])
                last.then_inc(oT_ps, 1)

            rounds(pe, slot)
            ranks(1, 2 * NG - 2, 0)
            o_transposes(NG - 1, 0)
            pe.wait_ge(xn_first, 2)
            xn_transposes(GATE, 2 * NG - 1, 7)
            gate_logits(2 * NG - 1)
            ranks(1, 2 * NG - 1, 1)
            totals(1)
            pe.wait_ge(routed[1], 1)
            experts(1)


_INS = ["L0_attn_x", "L0_attn_context", "L0_attn_Wq", "L0_attn_Wk", "L0_attn_Wv", "L0_attn_Wout", "L0_attn_bout",
        "L0_ffn_gate_w", "L0_ffn_gate_b", "L0_ffn_expert_bias", "L0_ffn_w1", "L0_ffn_b1", "L0_ffn_w2", "L0_ffn_b2"]


def kernel(**inputs):
    import numpy as _np
    import concourse.bacc as _bacc
    from concourse import mybir as _mybir
    from concourse.bass_utils import run_bass_kernel_spmd as _run

    nc = _bacc.Bacc("TRN2", target_bir_lowering=False, num_devices=1)
    arrays, args = {}, []
    for name in _INS:
        a = _np.ascontiguousarray(inputs[name])
        arrays[f"in_{name}"] = a
        args.append(nc.dram_tensor(f"in_{name}", a.shape, _mybir.dt.from_np(a.dtype), kind="ExternalInput").ap())
    shape = tuple(inputs["L0_attn_x"].shape)
    out = nc.dram_tensor("out_0", shape, _mybir.dt.float32, kind="ExternalOutput").ap()
    macaron_kernel(nc, *args, out)
    r = _run(nc, [arrays], core_ids=[0])
    return r.results[0]["out_0"]
```
